# Optimizing a Trainium2 kernel written in Bass

```python
import numpy as np
import jax
import jax.numpy as jnp

def _softmax(x, axis=-1):
    return jax.nn.softmax(x, axis=axis)

def _gelu(x):
    return jax.nn.gelu(x, approximate=True)

def _silu(x):
    return jax.nn.silu(x)

def _sigmoid(x):
    return jax.nn.sigmoid(x)

def _layernorm(x, axis=-1, eps=1e-05):
    m = jnp.mean(x, axis=axis, keepdims=True)
    v = jnp.var(x, axis=axis, keepdims=True)
    return (x - m) / jnp.sqrt(v + eps)

def _scatter_add(tgt, idx, src, axis=0):
    return tgt.at[idx].add(src)

def _segment_sum(src, seg, n):
    return jax.ops.segment_sum(src, seg, n)
kernel_name = 'mk_xattn_ffn_d1_seqx_r8_8edb69'

def setup_inputs(seed: int=0):
    np.random.seed(seed)
    _w = jnp.asarray

    def _rec_inputs():
        import jax
        import jax.numpy as jnp
        _rk = jax.random.key(seed)
        x = -0.0005207 + 1.001 * jax.random.normal(jax.random.fold_in(_rk, 1), (4, 256, 128), jnp.float32)
        _lenS = 256 - jax.random.randint(jax.random.fold_in(_rk, 7), (4,), 0, max(1, 256 // 4) + 1, jnp.int32)
        _lenS2 = 512 - jax.random.randint(jax.random.fold_in(_rk, 8), (4,), 0, max(1, 512 // 4) + 1, jnp.int32)
        _ctx_1024P = jax.random.normal(jax.random.fold_in(_rk, 11), (4, 16, 128), jnp.float32)
        _ctx_1024c = jax.random.dirichlet(jax.random.fold_in(_rk, 511), 0.3 * jnp.ones((16,), jnp.float32), (4, 512))
        _ctx_1024t = jnp.einsum('bsk,bkd->bsd', _ctx_1024c, _ctx_1024P)
        _ctx_1024t = _ctx_1024t * jax.lax.rsqrt(jnp.mean(jnp.square(_ctx_1024t)) + 1e-12) * 0.953939
        ctx_1024 = -1.52775e-05 + 0.999936 * (_ctx_1024t + 0.3 * jax.random.normal(jax.random.fold_in(_rk, 611), (4, 512, 128), jnp.float32))
        return (x, ctx_1024)
    x, ctx_1024 = _rec_inputs()

    def _L0_xattn_setup():
        import jax, jax.numpy as jnp
        import numpy as np
        DIM = 128
        HEADS = 16
        DHEAD = 64
        INNER = HEADS * DHEAD
        EPS = 1e-05

        def layer_norm(x, g, b):
            mu = jnp.mean(x, axis=-1, keepdims=True)
            var = jnp.mean(jnp.square(x - mu), axis=-1, keepdims=True)
            return (x - mu) * jax.lax.rsqrt(var + EPS) * g + b

        def apply_rope(x, cos, sin):
            d2 = x.shape[-1] // 2
            x1, x2 = (x[..., :d2], x[..., d2:])
            return jnp.concatenate([x1 * cos - x2 * sin, x2 * cos + x1 * sin], axis=-1)
        key = jax.random.key(seed)
        ks = jax.random.split(key, 10)
        B, N, S = (8, 32, 512)
        latents = jax.random.normal(ks[0], (B, N, DIM), dtype=jnp.float32)
        context = jax.random.normal(ks[1], (B, S, DIM), dtype=jnp.float32)
        cos = jax.random.uniform(ks[2], (S, DHEAD // 2), dtype=jnp.float32)
        sin = jax.random.uniform(ks[3], (S, DHEAD // 2), dtype=jnp.float32)
        init = lambda k, shp, fan_in: jax.random.normal(k, shp, dtype=jnp.float32) / np.sqrt(fan_in)
        return {'latents': latents, 'context': context, 'cos': cos, 'sin': sin, 'ln_lat_g': jnp.ones((DIM,), jnp.float32), 'ln_lat_b': jnp.zeros((DIM,), jnp.float32), 'ln_ctx_g': jnp.ones((DIM,), jnp.float32), 'ln_ctx_b': jnp.zeros((DIM,), jnp.float32), 'Wq': init(ks[4], (DIM, INNER), DIM), 'Wkv': init(ks[5], (DIM, 2 * INNER), DIM), 'Wo': init(ks[6], (INNER, DIM), INNER), 'bo': jnp.zeros((DIM,), jnp.float32)}
    _L0_xattn_all = _L0_xattn_setup()
    _L0_xattn_in = {k: v for k, v in _L0_xattn_all.items() if k in ('cos', 'sin', 'ln_lat_g', 'ln_lat_b', 'ln_ctx_g', 'ln_ctx_b', 'Wq', 'Wkv', 'Wo', 'bo')}
    del _L0_xattn_all

    def _L0_ffn_setup():
        import jax, jax.numpy as jnp
        import numpy as np
        S, B, H, F, E, K = (256, 2, 128, 256, 8, 2)

        def _moe_forward(hidden_states, router_w, w1, b1, w2, b2):
            s, b, h = hidden_states.shape
            T = s * b
            x = hidden_states.reshape(T, h)
            logits = jnp.einsum('th,eh->te', x, router_w)
            topk_logits, topk_idx = jax.lax.top_k(logits, K)
            probs = jax.nn.softmax(topk_logits, axis=-1)
            combine = jnp.zeros((T, E), dtype=x.dtype)
            combine = combine.at[jnp.arange(T)[:, None], topk_idx].add(probs.astype(x.dtype))
            hmid = jnp.einsum('th,efh->etf', x, w1) + b1[:, None, :]
            hmid = jax.nn.gelu(hmid, approximate=False)
            y = jnp.einsum('etf,ehf->eth', hmid, w2) + b2[:, None, :]
            out = jnp.einsum('eth,te->th', y, combine)
            return out.reshape(s, b, h)
        key = jax.random.key(seed)
        ks = jax.random.split(key, 6)
        std = 0.02
        return {'hidden_states': jax.random.normal(ks[0], (S, B, H), dtype=jnp.float32), 'router_w': jax.random.normal(ks[1], (E, H), dtype=jnp.float32) * std, 'w1': jax.random.normal(ks[2], (E, F, H), dtype=jnp.float32) * (1.0 / np.sqrt(H)), 'b1': jnp.zeros((E, F), dtype=jnp.float32), 'w2': jax.random.normal(ks[3], (E, H, F), dtype=jnp.float32) * (1.0 / np.sqrt(F)), 'b2': jnp.zeros((E, H), dtype=jnp.float32)}
    _L0_ffn_all = _L0_ffn_setup()
    _L0_ffn_in = {k: v for k, v in _L0_ffn_all.items() if k in ('router_w', 'w1', 'b1', 'w2', 'b2')}
    del _L0_ffn_all
    return {'x': x, 'ctx_1024': ctx_1024, 'L0_xattn_cos': _L0_xattn_in['cos'], 'L0_xattn_sin': _L0_xattn_in['sin'], 'L0_xattn_ln_lat_g': _L0_xattn_in['ln_lat_g'], 'L0_xattn_ln_lat_b': _L0_xattn_in['ln_lat_b'], 'L0_xattn_ln_ctx_g': _L0_xattn_in['ln_ctx_g'], 'L0_xattn_ln_ctx_b': _L0_xattn_in['ln_ctx_b'], 'L0_xattn_Wq': _L0_xattn_in['Wq'], 'L0_xattn_Wkv': _L0_xattn_in['Wkv'], 'L0_xattn_Wo': _L0_xattn_in['Wo'], 'L0_xattn_bo': _L0_xattn_in['bo'], 'L0_ffn_router_w': _L0_ffn_in['router_w'], 'L0_ffn_w1': _L0_ffn_in['w1'], 'L0_ffn_b1': _L0_ffn_in['b1'], 'L0_ffn_w2': _L0_ffn_in['w2'], 'L0_ffn_b2': _L0_ffn_in['b2']}

def reference(x, ctx_1024, L0_xattn_cos, L0_xattn_sin, L0_xattn_ln_lat_g, L0_xattn_ln_lat_b, L0_xattn_ln_ctx_g, L0_xattn_ln_ctx_b, L0_xattn_Wq, L0_xattn_Wkv, L0_xattn_Wo, L0_xattn_bo, L0_ffn_router_w, L0_ffn_w1, L0_ffn_b1, L0_ffn_w2, L0_ffn_b2):
    import jax
    import jax.numpy as jnp

    def _L0_xattn_ref(latents, context, cos, sin, ln_lat_g, ln_lat_b, ln_ctx_g, ln_ctx_b, Wq, Wkv, Wo, bo):
        import jax, jax.numpy as jnp
        import numpy as np
        DIM = 128
        HEADS = 16
        DHEAD = 64
        INNER = HEADS * DHEAD
        EPS = 1e-05

        def layer_norm(x, g, b):
            mu = jnp.mean(x, axis=-1, keepdims=True)
            var = jnp.mean(jnp.square(x - mu), axis=-1, keepdims=True)
            return (x - mu) * jax.lax.rsqrt(var + EPS) * g + b

        def apply_rope(x, cos, sin):
            d2 = x.shape[-1] // 2
            x1, x2 = (x[..., :d2], x[..., d2:])
            return jnp.concatenate([x1 * cos - x2 * sin, x2 * cos + x1 * sin], axis=-1)
        b, n, _ = latents.shape
        s = context.shape[1]
        lat = layer_norm(latents, ln_lat_g, ln_lat_b)
        ctx = layer_norm(context, ln_ctx_g, ln_ctx_b)
        q = (lat @ Wq).reshape(b, n, HEADS, DHEAD).transpose(0, 2, 1, 3)
        kv = ctx @ Wkv
        k, v = jnp.split(kv, 2, axis=-1)
        k = k.reshape(b, s, HEADS, DHEAD).transpose(0, 2, 1, 3)
        v = v.reshape(b, s, HEADS, DHEAD).transpose(0, 2, 1, 3)
        k = apply_rope(k, cos[None, None], sin[None, None])
        scale = DHEAD ** (-0.5)
        attn = jnp.einsum('bhnd,bhsd->bhns', q, k) * scale
        attn = jnp.clip(attn, -11.0, 11.0)
        attn = jax.nn.softmax(attn, axis=-1)
        out = jnp.einsum('bhns,bhsd->bhnd', attn, v)
        out = out.transpose(0, 2, 1, 3).reshape(b, n, INNER)
        return out @ Wo + bo

    def _L0_ffn_ref(hidden_states, router_w, w1, b1, w2, b2):
        import jax, jax.numpy as jnp
        import numpy as np
        S, B, H, F, E, K = (256, 2, 128, 256, 8, 2)

        def _moe_forward(hidden_states, router_w, w1, b1, w2, b2):
            s, b, h = hidden_states.shape
            T = s * b
            x = hidden_states.reshape(T, h)
            logits = jnp.einsum('th,eh->te', x, router_w)
            topk_logits, topk_idx = jax.lax.top_k(logits, K)
            probs = jax.nn.softmax(topk_logits, axis=-1)
            combine = jnp.zeros((T, E), dtype=x.dtype)
            combine = combine.at[jnp.arange(T)[:, None], topk_idx].add(probs.astype(x.dtype))
            hmid = jnp.einsum('th,efh->etf', x, w1) + b1[:, None, :]
            hmid = jax.nn.gelu(hmid, approximate=False)
            y = jnp.einsum('etf,ehf->eth', hmid, w2) + b2[:, None, :]
            out = jnp.einsum('eth,te->th', y, combine)
            return out.reshape(s, b, h)
        return _moe_forward(hidden_states, router_w, w1, b1, w2, b2)
    x = x + _L0_xattn_ref(_layernorm(x, axis=-1), ctx_1024, L0_xattn_cos, L0_xattn_sin, L0_xattn_ln_lat_g, L0_xattn_ln_lat_b, L0_xattn_ln_ctx_g, L0_xattn_ln_ctx_b, L0_xattn_Wq, L0_xattn_Wkv, L0_xattn_Wo, L0_xattn_bo)
    x = x + _L0_ffn_ref(_layernorm(x, axis=-1), L0_ffn_router_w, L0_ffn_w1, L0_ffn_b1, L0_ffn_w2, L0_ffn_b2)
    return x

_drawn_inputs = setup_inputs


def setup_inputs(seed=0):
    import zlib

    import numpy as np

    out = dict(_drawn_inputs(seed))
    spreads = {'L0_xattn_ln_lat_g': (1.0, 0.2),
     'L0_xattn_ln_lat_b': (0.0, 0.1),
     'L0_xattn_ln_ctx_g': (1.0, 0.2),
     'L0_xattn_ln_ctx_b': (0.0, 0.1),
     'L0_xattn_bo': (0.0, 0.1),
     'L0_ffn_b1': (0.0, 0.1),
     'L0_ffn_b2': (0.0, 0.1)}
    factors = {}
    for name, (base, spread) in spreads.items():
        noise = np.random.default_rng([zlib.crc32(name.encode()), seed]).standard_normal(out[name].shape)
        drawn = base * np.exp(spread * noise) if base else spread * noise
        out[name] = jnp.asarray(drawn.astype(out[name].dtype))
    for name, factor in factors.items():
        out[name] = (out[name] * factor).astype(out[name].dtype)
    return out
```

```python
from contextlib import ExitStack

import numpy as np

import concourse.bass as bass
from concourse import mybir

F32 = mybir.dt.float32
F32R = mybir.dt.float32r
U32 = mybir.dt.uint32
ALU = mybir.AluOpType
ACT = mybir.ActivationFunctionType

P = 128
B = 4
NQ = 256
NK = 512
D = 128
HEADS = 16
DH = 64
INNER = HEADS * DH
G = 4
GH = HEADS // G
PAIRS = HEADS // 2
KT = NK // P
QT = NQ // P
TOK = B * NQ
TT = TOK // P
E = 8
FF = 256
FT = E * FF // P
CH = 512
CHUNKS = TOK // CH
EPS = 1e-5
CLIP = 11.0
E_MIN = float(np.exp(np.float32(-CLIP)))
E_MAX = float(np.exp(np.float32(CLIP)))
SCALE = DH ** -0.5

WK_HI, WK_LO, WQ_HI, WQ_LO, WV_HI, WV_LO = (INNER * n for n in range(6))
W1_HI, W1_LO, W2_HI, W2_LO = (E * FF * n for n in range(4))

C_ID = 0
C_SEL = C_ID + P
C_HEAD = C_SEL + G * 32
C_EXP = C_HEAD + PAIRS * P
C_IOTA = C_EXP + E * P
C_ALL = C_IOTA + TT * E


def constants():
    c = np.zeros((P, C_ALL), np.float32)
    c[:, C_ID:C_ID + P] = np.eye(P, dtype=np.float32)
    for g in range(G):
        c[:, C_SEL + 32 * g + g] = 1
    c[:, C_SEL + G:C_SEL + 32] = 1
    for h in range(HEADS):
        row, at = 32 * (h % GH) + h // GH, C_HEAD + (h // 2) * P + (h % 2) * DH
        c[row, at:at + DH] = 1
    for e in range(E):
        c[e, C_EXP + e * P:C_EXP + (e + 1) * P] = 1
        c[E + e, C_EXP + e * P:C_EXP + (e + 1) * P] = 1
    c[:, C_IOTA:] = np.tile(np.arange(E, dtype=np.float32), TT)
    return c


SEED = 4


class Chain:

    def __init__(self, eng, sem, per_round):
        self.eng, self.sem, self.per, self.n, self.base = eng, sem, per_round, 0, 0

    def start(self, round_):
        self.base, self.n = round_ * self.per, 0

    def put(self, ins):
        self.n += 1
        ins.then_inc(self.sem, 1)

    def wait(self):
        self.eng.wait_ge(self.sem, self.base + self.n)

    def link(self, ins):
        self.put(ins)
        self.wait()

    def end(self):
        assert self.n == self.per, (self.n, self.per)


def first(r):
    return isinstance(r, int) and r == 0


def build(nc, x, ctx_in, cos_t, sin_t, vecs, wk, wq, wv, wo, bo, router_t, w1_t, b1_t, w2_t, b2, consts, out):
    stack = ExitStack()
    k_scratch = nc.dram_tensor("k_scratch", [G, GH, P, NK], F32, kind="Internal").ap()
    q_scratch = nc.dram_tensor("q_scratch", [G, GH, DH, NQ], F32, kind="Internal").ap()
    with stack:
        def sb(name, shape, dt=F32):
            return stack.enter_context(nc.sbuf_tensor(name, shape, dt))

        def sem(name):
            return stack.enter_context(nc.semaphore(name))

        w_split = sb("w_split", [P, 4 * E * FF], F32R)
        wo_sb = sb("wo_sb", [P, PAIRS, D])
        k_stack = sb("k_stack", [P, HEADS, NK], F32R)
        q_dup = sb("q_dup", [P, HEADS, NQ], F32R)
        q_lo = sb("q_lo", [P, PAIRS, NQ], F32R)
        v_sb = sb("v_sb", [P, KT, INNER])
        e_raw = sb("e_raw", [P, 2, KT * NQ])
        e_clip = sb("e_clip", [P, 4, KT * NQ])
        half_sum = sb("half_sum", [P, 2 * NQ])
        key_sum = sb("key_sum", [P, 8, NQ])
        rope_c = sb("rope_c", [P, 2, NK])
        rope_s = sb("rope_s", [P, 2, NK])
        k_hi = sb("k_hi", [P, 2, NK], F32R)
        k_lo = sb("k_lo", [P, 2, NK], F32R)
        q_hi = sb("q_hi", [P, 2, NQ], F32R)
        c_norm = sb("c_norm", [P, KT, D])
        x_norm = sb("x_norm", [P, QT, D])
        cT = sb("cT", [P, NK])
        cT_hi = sb("cT_hi", [P, NK], F32R)
        cT_lo = sb("cT_lo", [P, NK], F32R)
        xT = sb("xT", [P, NQ])
        xT_hi = sb("xT_hi", [P, NQ], F32R)
        xT_lo = sb("xT_lo", [P, NQ], F32R)
        o_sb = sb("o_sb", [P, PAIRS, NQ])
        recip = sb("recip", [P, NQ])
        recip_hi = sb("recip_hi", [P, NQ], F32R)
        recip_lo = sb("recip_lo", [P, NQ], F32R)
        x_all = sb("x_all", [P, TT, D])
        ctx_all = sb("ctx_all", [P, B * KT, D])
        cos_sb = sb("cos_sb", [P, NK])
        sin_sb = sb("sin_sb", [P, NK])
        bo_sb = sb("bo_sb", [P, D])
        vec_sb = sb("vec_sb", [P, 4])
        b1_sb = sb("b1_sb", [P, FT])
        router_sb = sb("router_sb", [P, E])
        b2_sb = sb("b2_sb", [2 * E, D])
        ident = sb("ident", [P, P])
        sel_sum = sb("sel_sum", [P, G, 32])
        sel_head = sb("sel_head", [P, PAIRS, P], F32R)
        iota = sb("iota", [P, TT, E])
        stats = sb("stats", [P, TT, 6])
        mv = sb("mv", [P, TT, 2])
        var_eps = sb("var_eps", [P, TT])
        rstd = sb("rstd", [P, TT])
        scrap = sb("scrap", [P, 1])
        minus_half = sb("minus_half", [P, TT])
        max8 = sb("max8", [P, TT, E])
        idx8 = sb("idx8", [P, TT, E], U32)
        idx_f = sb("idx_f", [P, TT, 2])
        top = sb("top", [P, 5, TT])
        one1 = sb("one1", [P, TT, E])
        one2 = sb("one2", [P, TT, E])
        comb = sb("comb", [P, TT, 2 * E])
        w_raw = e_clip
        head_raw = rope_c[:, :, :].rearrange("p a b -> p (a b)")
        h_norm = v_sb[:, 0, :].rearrange("p (t d) -> p t d", t=TT)
        hT = e_raw[:, 0, :]
        hT_hi = q_dup[:, 0:4, :].rearrange("p a b -> p (a b)")
        hT_lo = q_dup[:, 4:8, :].rearrange("p a b -> p (a b)")
        combT = k_stack[0:2 * E, 0:2, :].rearrange("p a b -> p (a b)")
        exp_raw = rope_s[0:2 * E, :, :].rearrange("p a b -> p (a b)")
        sel_exp = k_stack[0:2 * E, 2:4, :].rearrange("p a b -> p (a b)")
        b2_hi = k_stack[0:2 * E, 8, 0:D]
        b2_lo = k_stack[0:2 * E, 8, D:2 * D]
        logits = xT[:, 0:TT * E].rearrange("p (t e) -> p t e", t=TT)
        mid_hi = k_stack[:, 4:6, :]
        mid_lo = k_stack[:, 6:8, :]
        act_out = v_sb[:, 1, :].rearrange("p (a b) -> p a b", a=2)
        mid = v_sb[:, 2, :].rearrange("p (a b) -> p a b", a=2)
        yT = v_sb[:, 3, 0:CH]
        y_out = v_sb[:, 3, CH:2 * CH].rearrange("p (t d) -> p t d", t=CH // P)

        ps = [stack.enter_context(nc.psum_tensor(f"ps{n}", [P, 2, 512], F32)) for n in range(4)]

        def bank(n):
            return ps[n // 2][:, n % 2, :]

        in_first = sem("in_first")
        in_w = sem("in_w")
        in_rest = sem("in_rest")
        in_w12 = sem("in_w12")
        w_hi_done = sem("w_hi_done")
        w_lo_done = sem("w_lo_done")
        sel_done = sem("sel_done")
        const_done = sem("const_done")
        dve_prep = sem("dve_prep")
        var_done = sem("var_done")
        rstd_done = sem("rstd_done")
        norm_done = sem("norm_done")
        normT_done = sem("normT_done")
        split_done = sem("split_done")
        k_filled = sem("k_filled")
        k_taken = sem("k_taken")
        rope_done = sem("rope_done")
        k_hi_done = sem("k_hi_done")
        k_lo_done = sem("k_lo_done")
        k_stored = sem("k_stored")
        k_loaded = [sem(f"k_loaded{g}") for g in range(G)]
        q_filled = sem("q_filled")
        q_hi_done = sem("q_hi_done")
        q_lo_done = sem("q_lo_done")
        q_stored = sem("q_stored")
        q_loaded = [sem(f"q_loaded{g}") for g in range(G)]
        v_filled = sem("v_filled")
        v_done = sem("v_done")
        scores_done = sem("scores_done")
        exp_done = sem("exp_done")
        clip_done = sem("clip_done")
        half_done = sem("half_done")
        ksum_done = sem("ksum_done")
        pv_done = sem("pv_done")
        pv_taken = sem("pv_taken")
        sums_done = sem("sums_done")
        dve_attn = sem("dve_attn")
        recip_done = sem("recip_done")
        spread_done = sem("spread_done")
        scaled_done = sem("scaled_done")
        y_done = sem("y_done")
        resid_done = sem("resid_done")
        dve_moe = sem("dve_moe")
        mvar_done = sem("mvar_done")
        mrstd_done = sem("mrstd_done")
        hn_done = sem("hn_done")
        hT_filled = sem("hT_filled")
        hT_done = sem("hT_done")
        hT_hi_done = sem("hT_hi_done")
        hT_lo_done = sem("hT_lo_done")
        logits_done = sem("logits_done")
        gap_done = sem("gap_done")
        gap_exp = sem("gap_exp")
        comb_done = sem("comb_done")
        combT_filled = sem("combT_filled")
        combT_done = sem("combT_done")
        b2_done = sem("b2_done")
        w12_hi_done = sem("w12_hi_done")
        w12_lo_done = sem("w12_lo_done")
        cb_filled = sem("cb_filled")
        up_done = sem("up_done")
        gelu_done = sem("gelu_done")
        mid_done = sem("mid_done")
        mid_hi_done = sem("mid_hi_done")
        mid_lo_done = sem("mid_lo_done")
        down_done = sem("down_done")
        yT_done = sem("yT_done")
        yTT_done = sem("yTT_done")
        final_done = sem("final_done")
        stored = sem("stored")

        block = stack.enter_context(nc.Block())

        def flat(ap):
            return ap.rearrange("p a b -> p (a b)")

        @block.sync
        def _(sp):
            sp.dma_start(ctx_all[:, 0:KT, :], ctx_in[0].rearrange("(t p) d -> p t d", p=P)).then_inc(in_first, 16)
            sp.dma_start(x_all[:, 0:QT, :], x[0].rearrange("(t p) d -> p t d", p=P)).then_inc(in_first, 16)
            sp.dma_start(w_raw[:, 0, :], wk).then_inc(in_w, 16)
            sp.dma_start(ident[:], consts[:, C_ID:C_ID + P]).then_inc(in_first, 16)
            sp.dma_start(vec_sb[:], vecs).then_inc(in_first, 16)
            sp.dma_start(w_raw[:, 1, :], wq).then_inc(in_w, 16)
            sp.dma_start(w_raw[:, 2, :], wv).then_inc(in_w, 16)
            rest = [
                (head_raw, consts[:, C_HEAD:C_HEAD + PAIRS * P]),
                (cos_sb[:], cos_t), (sin_sb[:], sin_t),
                (sel_sum[:].rearrange("p g m -> p (g m)"), consts[:, C_SEL:C_SEL + G * 32]),
                (ctx_all[:, KT:, :], ctx_in[1:].rearrange("b (t p) d -> p (b t) d", p=P)),
                (x_all[:, QT:, :], x[1:].rearrange("b (t p) d -> p (b t) d", p=P)),
                (wo_sb[:], wo.rearrange("(c p) n -> p c n", p=P)),
                (bo_sb[:], bo.partition_broadcast(P)),
                (iota[:].rearrange("p t e -> p (t e)"), consts[:, C_IOTA:C_IOTA + TT * E]),
                (b1_sb[:], b1_t), (router_sb[:], router_t), (b2_sb[0:E, :], b2), (b2_sb[E:2 * E, :], b2),
            ]
            assert len(rest) == REST
            for dst, src in rest:
                sp.dma_start(dst, src).then_inc(in_rest, 16)

            def move_group(nb, g):
                done = nb * G + g
                sp.wait_ge(q_hi_done, done + 1)
                sp.dma_start(q_scratch[g].rearrange("(a h) d q -> (h d) a q", a=2),
                             q_hi[:].bitcast(F32)).then_inc(q_stored, 16)
                for part, hi, ready in ((k_hi, True, k_hi_done), (k_lo, False, k_lo_done)):
                    sp.wait_ge(ready, done + 1)
                    for odd in range(2):
                        at = 0 if hi != bool(odd) else DH
                        dst = k_scratch[g].rearrange("(jj jo) r s -> jo jj r s", jo=2)[odd, :, at:at + DH, :]
                        sp.dma_start(dst.rearrange("jj (r x) s -> jj r (x s)", x=2),
                                     flat(part[DH * odd:DH * odd + DH, :, :]).bitcast(F32)).then_inc(k_stored, 16)
                sp.wait_ge(q_stored, (done + 1) * 16)
                heads = slice(g * GH, (g + 1) * GH)
                for side in range(2):
                    sp.dma_start(q_dup[DH * side:DH * side + DH, heads, :].bitcast(F32),
                                 q_scratch[g].rearrange("h d q -> d h q")).then_inc(q_loaded[g], 16)
                sp.wait_ge(k_stored, (done + 1) * 64)
                sp.dma_start(k_stack[:, heads, :].bitcast(F32),
                             k_scratch[g].rearrange("h r s -> r h s")).then_inc(k_loaded[g], 16)

            for g in range(G):
                move_group(0, g)

            with sp.Fori(1, B) as nb:
                for g in range(G):
                    move_group(nb, g)

            sp.wait_ge(pv_done, SEED + B * PAIRS)
            sp.wait_ge(ksum_done, SEED + B * HEADS)
            sp.dma_start(w_raw[:, 0:2, :].rearrange("p a b -> p (a b)"), w1_t).then_inc(in_w12, 16)
            sp.dma_start(w_raw[:, 2:4, :].rearrange("p a b -> p (a b)"), w2_t).then_inc(in_w12, 16)
            sp.dma_start(exp_raw, consts[0:2 * E, C_EXP:C_EXP + E * P]).then_inc(in_w12, 16)
            for c in range(CHUNKS):
                sp.wait_ge(final_done, c + 1)
                sp.dma_start(out[c * CH // NQ:(c + 1) * CH // NQ].rearrange("b (t p) d -> p (b t) d", p=P),
                             y_out).then_inc(stored, 16)
            sp.wait_ge(stored, 16 * CHUNKS)

        @block.tensor
        def _(pe):
            mm = nc.tensor.matmul
            for freed in (pv_done, sums_done):
                pe.sem_inc(freed, SEED)

            def three(dst, w, w_lo, m, m_lo, start=True, stop=True):
                mm(dst, w, m, start=start, stop=False)
                mm(dst, w_lo, m, start=False, stop=False)
                return mm(dst, w, m_lo, start=False, stop=stop)

            def norm_transposes(nb):
                pe.wait_ge(norm_done, nb * 2 + 1)
                if not first(nb):
                    pe.wait_ge(v_done, nb * 2 * G)
                    pe.wait_ge(resid_done, SEED + nb - 1)
                    pe.wait_ge(scaled_done, SEED + nb * 4 - 4)
                for t in range(KT):
                    ins = nc.tensor.transpose(bank(6)[:, t * P:(t + 1) * P], c_norm[:, t, :], ident[:])
                ins.then_inc(normT_done, 1)
                pe.wait_ge(norm_done, nb * 2 + 2)
                for t in range(QT):
                    ins = nc.tensor.transpose(bank(7)[:, t * P:(t + 1) * P], x_norm[:, t, :], ident[:])
                ins.then_inc(normT_done, 1)

            def keys(nb, g):
                if g == 0:
                    pe.wait_ge(split_done, nb * 2 + 2)
                else:
                    pe.wait_ge(v_done, nb * 2 * G + 2 * g)
                for half in range(2):
                    at = (2 * g + half) * P
                    ins = three(bank(6 + half), w_split[:, WK_HI + at:WK_HI + at + P],
                                w_split[:, WK_LO + at:WK_LO + at + P], cT_hi[:], cT_lo[:])
                ins.then_inc(k_filled, 1)

            def queries(nb, g):
                pe.wait_ge(k_taken, nb * G + g + 1)
                for pair in range(2):
                    at = (2 * g + pair) * P
                    ins = three(bank(6)[:, pair * NQ:(pair + 1) * NQ], w_split[:, WQ_HI + at:WQ_HI + at + P],
                                w_split[:, WQ_LO + at:WQ_LO + at + P], xT_hi[:], xT_lo[:])
                ins.then_inc(q_filled, 1)

            def values(nb, g, half):
                if half == 0:
                    pe.wait_ge(k_taken, nb * G + g + 1)
                else:
                    pe.wait_ge(q_lo_done, nb * G + g + 1)
                n = GH * DH
                for t in range(2):
                    kt = 2 * half + t
                    w = slice(WV_HI + g * n, WV_HI + (g + 1) * n)
                    w_lo = slice(WV_LO + g * n, WV_LO + (g + 1) * n)
                    ins = three(bank(7 - half)[:, t * n:(t + 1) * n], cT_hi[:, kt * P:(kt + 1) * P],
                                cT_lo[:, kt * P:(kt + 1) * P], w_split[:, w], w_split[:, w_lo])
                ins.then_inc(v_filled, 1)

            def scores(b, h):
                g, odd = h // GH, h % 2
                if h % GH == 0:
                    pe.wait_ge(k_loaded[g], b * 16 + 16)
                    pe.wait_ge(q_loaded[g], b * 32 + 32)
                    pe.wait_ge(q_lo_done, b * G + g + 1)
                pe.wait_ge(exp_done, SEED + b * HEADS + h - 1)
                hi_rows = slice(DH * odd, DH * odd + DH)
                for kt in range(KT):
                    dst = bank(2 * (h % 2) + kt // 2)[:, (kt % 2) * NQ:(kt % 2) * NQ + NQ]
                    keys_ = slice(kt * P, (kt + 1) * P)
                    mm(dst, k_stack[:, h, keys_], q_dup[:, h, :], start=True, stop=False)
                    ins = mm(dst, k_stack[hi_rows, h, keys_], q_lo[hi_rows, h // 2, :], start=False, stop=True)
                ins.then_inc(scores_done, 1)

            def weigh(b, pair):
                if pair % 2 == 0:
                    pe.wait_ge(v_done, b * 2 * G + 2 * (pair // 2) + 2)
                pe.wait_ge(clip_done, SEED + b * HEADS + 2 * pair + 2)
                pe.wait_ge(pv_taken, SEED + b * PAIRS + pair)
                for kt in range(KT):
                    for odd in range(2):
                        h = 2 * pair + odd
                        ins = mm(bank(4)[DH * odd:DH * odd + DH, 0:NQ], v_sb[:, kt, h * DH:(h + 1) * DH],
                                 e_clip[:, h % 4, kt * NQ:(kt + 1) * NQ], start=(kt == 0), stop=(kt == KT - 1))
                ins.then_inc(pv_done, 1)

            def sums(b, g):
                pe.wait_ge(ksum_done, SEED + b * HEADS + (g + 1) * GH)
                if g == 0:
                    pe.wait_ge(recip_done, SEED + b)
                for j in range(GH):
                    ins = mm(bank(5)[32 * j:32 * j + 32, 0:NQ], sel_sum[:, g, :], key_sum[:, (g * GH + j) % 8, :],
                             start=(g == 0), stop=(g == G - 1))
                ins.then_inc(sums_done, 1)

            def spread(b, k):
                if k >= 2:
                    pe.wait_ge(scaled_done, SEED + b * 4 + k - 1)
                for pair in (2 * k, 2 * k + 1):
                    dst = bank(6 + k % 2)[:, (pair % 2) * NQ:(pair % 2) * NQ + NQ]
                    mm(dst, sel_head[:, pair, :], recip_hi[:], start=True, stop=False)
                    ins = mm(dst, sel_head[:, pair, :], recip_lo[:], start=False, stop=True)
                ins.then_inc(spread_done, 1)

            def project(b):
                pe.wait_ge(scaled_done, SEED + b * 4 + 4)
                for t in range(QT):
                    for pair in range(PAIRS):
                        ins = mm(bank(6)[:, t * D:(t + 1) * D], o_sb[:, pair, t * P:(t + 1) * P], wo_sb[:, pair, :],
                                 start=(pair == 0), stop=(pair == PAIRS - 1))
                ins.then_inc(y_done, 1)

            def batch(b, nb):
                for p in range(PAIRS + 1):
                    even = p % 2 == 0
                    if nb is not None and even and p >= 2:
                        keys(nb, p // 2 - 1)
                    if nb is not None and not even and p >= 3:
                        values(nb, (p - 3) // 2, 0)
                    if p < PAIRS:
                        scores(b, 2 * p)
                        scores(b, 2 * p + 1)
                    if p >= 1:
                        weigh(b, p - 1)
                    if not even and p >= 3:
                        sums(b, (p - 3) // 2)
                        if nb is not None:
                            values(nb, (p - 3) // 2, 1)
                    if nb is not None and p == 1:
                        norm_transposes(nb)
                    if nb is not None and even and p >= 2:
                        queries(nb, p // 2 - 1)
                sums(b, G - 1)
                if nb is not None:
                    values(nb, G - 1, 0)
                    values(nb, G - 1, 1)
                    pe.wait_ge(v_done, nb * 2 * G + 2 * G)
                pe.wait_ge(recip_done, SEED + b + 1)
                for k in range(4):
                    spread(b, k)
                project(b)

            pe.wait_ge(in_first, 64)
            norm_transposes(0)
            pe.wait_ge(w_hi_done, 3)
            pe.wait_ge(w_lo_done, 3)
            for g in range(G):
                keys(0, g)
                queries(0, g)
                values(0, g, 0)
                values(0, g, 1)
            pe.wait_ge(in_rest, REST * 16)
            pe.wait_ge(sel_done, 1)
            with pe.Fori(0, B - 1) as b:
                batch(b, b + 1)
            batch(B - 1, None)

            pe.wait_ge(hn_done, 1)
            for t in range(TT):
                ins = nc.tensor.transpose(bank(t // 4)[:, (t % 4) * P:(t % 4 + 1) * P], h_norm[:, t, :], ident[:])
            ins.then_inc(hT_filled, 1)
            pe.wait_ge(hT_done, 1)
            for t in range(TT):
                ins = mm(bank(4)[:, t * E:(t + 1) * E], hT[:, t * P:(t + 1) * P], router_sb[:],
                         start=True, stop=True)
            ins.then_inc(logits_done, 1)
            pe.wait_ge(comb_done, 1)
            for t in range(TT):
                ins = nc.tensor.transpose(bank(t // 4)[0:2 * E, (t % 4) * P:(t % 4 + 1) * P], comb[:, t, :], ident[:])
            ins.then_inc(combT_filled, 1)
            pe.wait_ge(combT_done, 1)
            pe.wait_ge(hT_lo_done, 1)
            pe.wait_ge(w12_hi_done, 2)
            pe.wait_ge(w12_lo_done, 2)
            pe.wait_ge(b2_done, 1)

            for c in range(CHUNKS):
                tok = slice(c * CH, (c + 1) * CH)

                def up(f):
                    n = c * FT + f
                    e = f // 2
                    if f % 2 == 0:
                        if c * E + e >= 2:
                            pe.wait_ge(mid_done, 2 * (c * E + e - 1))
                        mm(bank(1 + e % 2), sel_exp[:, e * P:(e + 1) * P], combT[:, tok],
                           start=True, stop=True).then_inc(cb_filled, 1)
                    if n >= 4:
                        pe.wait_ge(gelu_done, n - 3)
                    three(bank(3 + f % 4), w_split[:, W1_HI + f * P:W1_HI + (f + 1) * P],
                          w_split[:, W1_LO + f * P:W1_LO + (f + 1) * P],
                          hT_hi[:, tok], hT_lo[:, tok]).then_inc(up_done, 1)

                def down(f):
                    n = c * FT + f
                    pe.wait_ge(mid_lo_done, n + 1)
                    three(bank(0), w_split[:, W2_HI + f * P:W2_HI + (f + 1) * P],
                          w_split[:, W2_LO + f * P:W2_LO + (f + 1) * P],
                          mid_hi[:, f % 2, :], mid_lo[:, f % 2, :], start=False, stop=(f == FT - 1)).then_inc(down_done, 1)

                if c:
                    pe.wait_ge(yT_done, c)
                mm(bank(0), b2_hi, combT[:, tok], start=True, stop=False)
                mm(bank(0), b2_lo, combT[:, tok], start=False, stop=False)
                for f in range(FT + LAG):
                    if f < FT:
                        up(f)
                    if f >= LAG:
                        down(f - LAG)
                pe.wait_ge(yT_done, c + 1)
                for t in range(CH // P):
                    ins = nc.tensor.transpose(bank(7)[:, t * P:(t + 1) * P], yT[:, t * P:(t + 1) * P], ident[:])
                ins.then_inc(yTT_done, 1)

        @block.scalar
        def _(act):
            copy = nc.scalar.copy
            for freed in (exp_done, pv_taken):
                act.sem_inc(freed, SEED)

            def keys_hi(nb, g):
                act.wait_ge(rope_done, nb * G + g + 1)
                if not (first(nb) and g == 0):
                    act.wait_ge(k_stored, (nb * G + g) * 64)
                copy(flat(k_hi[:]), flat(rope_c[:])).then_inc(k_hi_done, 1)

            def queries_hi(nb, g):
                act.wait_ge(q_filled, nb * G + g + 1)
                if not (first(nb) and g == 0):
                    act.wait_ge(q_stored, (nb * G + g) * 16)
                copy(flat(q_hi[:]), bank(6)).then_inc(q_hi_done, 1)

            def values_out(nb, g, half):
                n = GH * DH
                act.wait_ge(v_filled, nb * 2 * G + 2 * g + half + 1)
                copy(v_sb[:, 2 * half:2 * half + 2, g * n:(g + 1) * n],
                     bank(7 - half).rearrange("p (t n) -> p t n", t=2)).then_inc(v_done, 1)

            def exps(b, h):
                act.wait_ge(scores_done, b * HEADS + h + 1)
                act.wait_ge(clip_done, SEED + b * HEADS + h - 1)
                nc.scalar.activation(e_raw[:, h % 2, :], flat(ps[h % 2][:, :, :]), ACT.Exp,
                                     scale=SCALE).then_inc(exp_done, 1)

            def take(b, pair):
                act.wait_ge(pv_done, SEED + b * PAIRS + pair + 1)
                copy(o_sb[:, pair, :], bank(4)[:, 0:NQ]).then_inc(pv_taken, 1)

            def batch(b, nb):
                for p in range(PAIRS + 1):
                    even = p % 2 == 0
                    if p < PAIRS:
                        exps(b, 2 * p)
                    if nb is not None and not even and p >= 3:
                        values_out(nb, (p - 3) // 2, 0)
                    if p < PAIRS:
                        exps(b, 2 * p + 1)
                    if p >= 1:
                        take(b, p - 1)
                    if nb is not None and even and p >= 2:
                        keys_hi(nb, p // 2 - 1)
                    if nb is not None and not even and p >= 3:
                        values_out(nb, (p - 3) // 2, 1)
                    if nb is not None and even and p >= 2:
                        queries_hi(nb, p // 2 - 1)
                if nb is not None:
                    values_out(nb, G - 1, 0)
                    values_out(nb, G - 1, 1)

            for n, at in enumerate((WK_HI, WQ_HI, WV_HI)):
                act.wait_ge(in_w, 48)
                copy(w_split[:, at:at + INNER], w_raw[:, n, :]).then_inc(w_hi_done, 1)
            for g in range(G):
                keys_hi(0, g)
                queries_hi(0, g)
                values_out(0, g, 0)
                values_out(0, g, 1)
            with act.Fori(0, B - 1) as b:
                batch(b, b + 1)
            batch(B - 1, None)

            act.wait_ge(in_w12, 48)
            act.wait_ge(y_done, B)
            copy(w_split[:, W1_HI:W1_HI + E * FF], w_raw[:, 0:2, :]).then_inc(w12_hi_done, 1)
            copy(w_split[:, W2_HI:W2_HI + E * FF], w_raw[:, 2:4, :]).then_inc(w12_hi_done, 1)
            act.wait_ge(hT_done, 1)
            copy(hT_hi, hT).then_inc(hT_hi_done, 1)
            act.wait_ge(gap_done, 1)
            nc.scalar.activation(top[:, 1, :], top[:, 0, :], ACT.Exp).then_inc(gap_exp, 1)
            act.wait_ge(combT_filled, 1)
            copy(combT, ps[0][0:2 * E, :, :].rearrange("p a b -> p (a b)")).then_inc(combT_done, 1)
            for c in range(CHUNKS):
                def gelu(f):
                    n = c * FT + f
                    act.wait_ge(up_done, n + 1)
                    if n >= 2:
                        act.wait_ge(mid_done, n - 1)
                    nc.scalar.activation(act_out[:, f % 2, :], bank(3 + f % 4), ACT.Gelu,
                                         bias=b1_sb[:, f:f + 1]).then_inc(gelu_done, 1)

                def part(f):
                    n = c * FT + f
                    act.wait_ge(mid_done, n + 1)
                    if n >= 2:
                        act.wait_ge(down_done, n - 1)
                    copy(mid_hi[:, f % 2, :], mid[:, f % 2, :]).then_inc(mid_hi_done, 1)

                for f in range(FT + 1):
                    if f < FT:
                        gelu(f)
                    if f >= 1:
                        part(f - 1)
                act.wait_ge(down_done, (c + 1) * FT)
                if c:
                    act.wait_ge(yTT_done, c)
                copy(yT, bank(0)).then_inc(yT_done, 1)

        @block.vector
        def _(dve):
            v = nc.vector
            for freed in (clip_done, recip_done, scaled_done, resid_done):
                dve.sem_inc(freed, SEED)
            prep = Chain(dve, dve_prep, PREP)
            attn = Chain(dve, dve_attn, ATTN)

            def norm_stats(chain, tiles, n, base=0):
                for t in range(n):
                    chain.put(v.bn_stats(stats[:, base + t, :], tiles[t]))
                chain.wait()
                chain.put(v.memset(scrap[:], 0.0))
                for t in range(n):
                    chain.put(v.bn_aggr(mv[:, base + t, :], stats[:, base + t, :]))
                chain.wait()
                return v.tensor_scalar(var_eps[:, base:base + n], mv[:, base:base + n, 1], EPS, None, ALU.add)

            def normalise(dst, src, t):
                return v.tensor_scalar(dst, src, mv[:, t, 0:1], rstd[:, t:t + 1], ALU.subtract, ALU.mult)

            def norms(nb):
                rows = [ctx_all[:, bass.ds(nb * KT + t, 1), :] for t in range(KT)]
                rows += [x_all[:, bass.ds(nb * QT + t, 1), :] for t in range(QT)]
                rows = [r.rearrange("p a d -> p (a d)") for r in rows]
                norm_stats(prep, rows, KT + QT).then_inc(var_done, 1)
                dve.wait_ge(rstd_done, nb * 2 + 1)
                for t in range(KT):
                    ins = normalise(c_norm[:, t, :], rows[t], t)
                    if t < KT - 1:
                        prep.put(ins)
                ins.then_inc(norm_done, 1)
                for t in range(QT):
                    prep.put(normalise(x_norm[:, t, :], rows[KT + t], KT + t))
                prep.wait()
                norm_stats(prep, [x_norm[:, t, :] for t in range(QT)], QT).then_inc(var_done, 1)
                dve.wait_ge(rstd_done, nb * 2 + 2)
                for t in range(QT):
                    ins = normalise(x_norm[:, t, :], x_norm[:, t, :], t)
                    if t < QT - 1:
                        prep.put(ins)
                ins.then_inc(norm_done, 1)

            def splits(nb):
                for n, (full, hi, lo, src, gain) in enumerate((
                        (cT, cT_hi, cT_lo, bank(6), 2), (xT, xT_hi, xT_lo, bank(7)[:, 0:NQ], 0))):
                    dve.wait_ge(normT_done, nb * 2 + n + 1)
                    prep.link(v.tensor_scalar(full[:], src, vec_sb[:, gain:gain + 1], vec_sb[:, gain + 1:gain + 2],
                                              ALU.mult, ALU.add))
                    prep.link(v.tensor_copy(hi[:], full[:]))
                    v.tensor_tensor(lo[:], full[:], hi[:].bitcast(F32), ALU.subtract).then_inc(split_done, 1)

            def rotate(nb, g):
                dve.wait_ge(k_filled, nb * G + g + 1)
                if not (first(nb) and g == 0):
                    dve.wait_ge(k_hi_done, nb * G + g)
                    dve.wait_ge(k_lo_done, nb * G + g)
                both = ps[3][:, :, :]
                prep.put(v.tensor_tensor(rope_c[:], both, cos_sb[:].unsqueeze(1).to_broadcast([P, 2, NK]), ALU.mult))
                v.tensor_tensor(rope_s[:], both, sin_sb[:].unsqueeze(1).to_broadcast([P, 2, NK]),
                                ALU.mult).then_inc(k_taken, 1)

            def rotate_sum(nb, g):
                prep.wait()
                dve.wait_ge(k_taken, nb * G + g + 1)
                prep.put(v.tensor_tensor(rope_c[:, 0, :], rope_c[:, 0, :], rope_s[:, 1, :], ALU.subtract))
                v.tensor_tensor(rope_c[:, 1, :], rope_c[:, 1, :], rope_s[:, 0, :], ALU.add).then_inc(rope_done, 1)

            def keys_lo(nb, g):
                dve.wait_ge(k_hi_done, nb * G + g + 1)
                dve.wait_ge(rope_done, nb * G + g + 1)
                prep.wait()
                if not (first(nb) and g == 0):
                    dve.wait_ge(k_stored, (nb * G + g) * 64)
                v.tensor_tensor(flat(k_lo[:]), flat(rope_c[:]), flat(k_hi[:]).bitcast(F32),
                                ALU.subtract).then_inc(k_lo_done, 1)

            def queries_lo(nb, g):
                dve.wait_ge(q_hi_done, nb * G + g + 1)
                v.tensor_tensor(flat(q_lo[:, 2 * g:2 * g + 2, :]), bank(6), flat(q_hi[:]).bitcast(F32),
                                ALU.subtract).then_inc(q_lo_done, 1)

            def clip(b, h):
                dve.wait_ge(exp_done, SEED + b * HEADS + h + 1)
                dve.wait_ge(pv_done, SEED + b * PAIRS + h // 2 - 1)
                dve.wait_ge(ksum_done, SEED + b * HEADS + h - 3)
                v.tensor_scalar(e_clip[:, h % 4, :], e_raw[:, h % 2, :], E_MIN, E_MAX, ALU.max,
                                ALU.min).then_inc(clip_done, 1)

            def reciprocals(b):
                attn.start(b)
                dve.wait_ge(sums_done, SEED + b * G + G)
                attn.link(v.reciprocal(recip[:], bank(5)[:, 0:NQ]))
                attn.link(v.tensor_copy(recip_hi[:], recip[:]))
                v.tensor_tensor(recip_lo[:], recip[:], recip_hi[:].bitcast(F32), ALU.subtract).then_inc(recip_done, 1)

            def scale(b):
                for k in range(4):
                    dve.wait_ge(spread_done, b * 4 + k + 1)
                    dve.wait_ge(pv_taken, SEED + b * PAIRS + 2 * k + 2)
                    o = flat(o_sb[:, 2 * k:2 * k + 2, :])
                    v.tensor_tensor(o, bank(6 + k % 2), o, ALU.mult).then_inc(scaled_done, 1)

            def residual(b):
                dve.wait_ge(y_done, b + 1)
                rows = x_all[:, bass.ds(b * QT, QT), :]
                attn.link(v.tensor_tensor(rows, bank(6)[:, 0:QT * D].rearrange("p (t d) -> p t d", t=QT), rows, ALU.add))
                v.tensor_tensor(rows, rows, bo_sb[:].unsqueeze(1).to_broadcast([P, QT, D]), ALU.add).then_inc(resid_done, 1)
                attn.end()

            def batch(b, nb):
                if nb is not None:
                    prep.start(nb)
                for p in range(PAIRS + 1):
                    even = p % 2 == 0
                    if p < PAIRS:
                        clip(b, 2 * p)
                    if nb is not None and p == 0:
                        norms(nb)
                    if nb is not None and even and p >= 2:
                        rotate(nb, p // 2 - 1)
                    if nb is not None and not even and p >= 3:
                        keys_lo(nb, (p - 3) // 2)
                        queries_lo(nb, (p - 3) // 2)
                    if p < PAIRS:
                        clip(b, 2 * p + 1)
                    if nb is not None and even and p >= 2:
                        rotate_sum(nb, p // 2 - 1)
                    if nb is not None and p == 1:
                        splits(nb)
                if nb is not None:
                    keys_lo(nb, G - 1)
                    queries_lo(nb, G - 1)
                    prep.end()
                reciprocals(b)
                scale(b)
                residual(b)

            dve.wait_ge(in_first, 64)
            dve.wait_ge(const_done, 1)
            prep.start(0)
            norms(0)
            splits(0)
            for n, (hi, lo) in enumerate(((WK_HI, WK_LO), (WQ_HI, WQ_LO), (WV_HI, WV_LO))):
                dve.wait_ge(w_hi_done, n + 1)
                v.tensor_tensor(w_split[:, lo:lo + INNER], w_raw[:, n, :], w_split[:, hi:hi + INNER].bitcast(F32),
                                ALU.subtract).then_inc(w_lo_done, 1)
            dve.wait_ge(in_rest, REST * 16)
            v.tensor_copy(flat(sel_head[:]), head_raw).then_inc(sel_done, 1)
            dve.wait_ge(w_lo_done, 3)
            dve.wait_ge(sel_done, 1)
            for g in range(G):
                rotate(0, g)
                rotate_sum(0, g)
                keys_lo(0, g)
                queries_lo(0, g)
            prep.end()
            with dve.Fori(0, B - 1) as b:
                batch(b, b + 1)
            batch(B - 1, None)

            moe = Chain(dve, dve_moe, 0)
            dve.wait_ge(resid_done, SEED + B)
            norm_stats(moe, [x_all[:, t, :] for t in range(TT)], TT).then_inc(mvar_done, 1)
            dve.wait_ge(mrstd_done, 1)
            for t in range(TT):
                ins = normalise(h_norm[:, t, :], x_all[:, t, :], t)
                if t < TT - 1:
                    moe.put(ins)
            ins.then_inc(hn_done, 1)
            dve.wait_ge(hT_filled, 1)
            v.tensor_copy(hT, flat(ps[0][:, :, :])).then_inc(hT_done, 1)
            dve.wait_ge(w12_hi_done, 2)
            for n, (hi, lo) in enumerate(((W1_HI, W1_LO), (W2_HI, W2_LO))):
                v.tensor_tensor(w_split[:, lo:lo + E * FF], flat(w_raw[:, 2 * n:2 * n + 2, :]),
                                w_split[:, hi:hi + E * FF].bitcast(F32), ALU.subtract).then_inc(w12_lo_done, 1)
            dve.wait_ge(logits_done, 1)
            moe.link(v.tensor_copy(flat(logits), bank(4)[:, 0:TT * E]))
            for t in range(TT):
                moe.put(v.max(max8[:, t, :], logits[:, t, :]))
            moe.wait()
            for t in range(TT):
                moe.put(v.max_index(idx8[:, t, :], max8[:, t, :], logits[:, t, :]))
            v.tensor_tensor(top[:, 0, :], max8[:, :, 1], max8[:, :, 0], ALU.subtract).then_inc(gap_done, 1)
            moe.wait()
            moe.put(v.tensor_copy(idx_f[:], idx8[:, :, 0:2]))
            dve.wait_ge(gap_exp, 1)
            moe.link(v.tensor_scalar(top[:, 2, :], top[:, 1, :], 1.0, None, ALU.add))
            moe.link(v.reciprocal(top[:, 3, :], top[:, 2, :]))
            moe.put(v.tensor_tensor(top[:, 4, :], top[:, 1, :], top[:, 3, :], ALU.mult))
            for n, one in enumerate((one1, one2)):
                moe.put(v.tensor_tensor(one[:], iota[:], idx_f[:, :, n:n + 1].to_broadcast([P, TT, E]), ALU.is_equal))
            moe.wait()
            for n, one in enumerate((one1, one2)):
                moe.put(v.tensor_tensor(one[:], one[:], top[:, 3 + n, :].unsqueeze(2).to_broadcast([P, TT, E]), ALU.mult))
            moe.wait()
            moe.link(v.tensor_tensor(one1[:], one1[:], one2[:], ALU.add))
            moe.link(v.tensor_copy(comb[:, :, 0:E].bitcast(F32R), one1[:]))
            v.tensor_tensor(comb[:, :, E:2 * E], one1[:], comb[:, :, 0:E], ALU.subtract).then_inc(comb_done, 1)
            dve.wait_ge(hT_hi_done, 1)
            v.tensor_tensor(hT_lo, hT, hT_hi.bitcast(F32), ALU.subtract).then_inc(hT_lo_done, 1)
            moe.put(v.tensor_copy(sel_exp, exp_raw))
            moe.link(v.tensor_copy(b2_hi, b2_sb[:]))
            v.tensor_tensor(b2_lo, b2_sb[:], b2_hi.bitcast(F32), ALU.subtract).then_inc(b2_done, 1)
            for c in range(CHUNKS):
                def weigh_mid(f):
                    n = c * FT + f
                    dve.wait_ge(gelu_done, n + 1)
                    dve.wait_ge(cb_filled, c * E + f // 2 + 1)
                    if n >= 2:
                        dve.wait_ge(mid_hi_done, n - 1)
                        dve.wait_ge(mid_lo_done, n - 1)
                    v.tensor_tensor(mid[:, f % 2, :], act_out[:, f % 2, :], bank(1 + (f // 2) % 2),
                                    ALU.mult).then_inc(mid_done, 1)

                def part(f):
                    n = c * FT + f
                    dve.wait_ge(mid_hi_done, n + 1)
                    if n >= 2:
                        dve.wait_ge(down_done, n - 1)
                    v.tensor_tensor(mid_lo[:, f % 2, :], mid[:, f % 2, :], mid_hi[:, f % 2, :].bitcast(F32),
                                    ALU.subtract).then_inc(mid_lo_done, 1)

                for f in range(FT + 1):
                    if f < FT:
                        weigh_mid(f)
                    if f >= 1:
                        part(f - 1)
                dve.wait_ge(yTT_done, c + 1)
                if c:
                    dve.wait_ge(stored, 16 * c)
                t0 = c * CH // P
                v.tensor_tensor(y_out, x_all[:, t0:t0 + CH // P, :], bank(7).rearrange("p (t d) -> p t d", d=D),
                                ALU.add).then_inc(final_done, 1)

        @block.gpsimd
        def _(pool):
            pool.sem_inc(ksum_done, SEED)
            nc.gpsimd.memset(minus_half[:], -0.5).then_inc(const_done, 1)
            pool.wait_ge(const_done, 1)

            def power(nb, n, tiles):
                pool.wait_ge(var_done, nb * 2 + n + 1)
                nc.gpsimd.tensor_tensor(rstd[:, 0:tiles], var_eps[:, 0:tiles], minus_half[:, 0:tiles],
                                        ALU.pow).then_inc(rstd_done, 1)

            def add_keys(b, h):
                pool.wait_ge(clip_done, SEED + b * HEADS + h + 1)
                pool.wait_ge(ksum_done, SEED + b * HEADS + h)
                pool.wait_ge(sums_done, SEED + b * G + h // GH - 1)
                n = 2 * NQ
                nc.gpsimd.tensor_tensor(half_sum[:], e_clip[:, h % 4, 0:n], e_clip[:, h % 4, n:2 * n],
                                        ALU.add).then_inc(half_done, 1)
                pool.wait_ge(half_done, b * HEADS + h + 1)
                nc.gpsimd.tensor_tensor(key_sum[:, h % 8, :], half_sum[:, 0:NQ], half_sum[:, NQ:n],
                                        ALU.add).then_inc(ksum_done, 1)

            def batch(b, nb):
                for h in range(HEADS):
                    add_keys(b, h)
                    if nb is not None and h == 0:
                        power(nb, 0, KT + QT)
                        power(nb, 1, QT)

            power(0, 0, KT + QT)
            power(0, 1, QT)
            with pool.Fori(0, B - 1) as b:
                batch(b, b + 1)
            batch(B - 1, None)
            pool.wait_ge(mvar_done, 1)
            nc.gpsimd.tensor_tensor(rstd[:], var_eps[:], minus_half[:], ALU.pow).then_inc(mrstd_done, 1)


REST = 13
LAG = 2
PREP = 36
ATTN = 3


def kernel(x, ctx_1024, L0_xattn_cos, L0_xattn_sin, L0_xattn_ln_lat_g, L0_xattn_ln_lat_b, L0_xattn_ln_ctx_g,
           L0_xattn_ln_ctx_b, L0_xattn_Wq, L0_xattn_Wkv, L0_xattn_Wo, L0_xattn_bo, L0_ffn_router_w, L0_ffn_w1,
           L0_ffn_b1, L0_ffn_w2, L0_ffn_b2):
    import concourse.bacc as bacc
    from concourse.bass_utils import run_bass_kernel_spmd

    f = lambda a: np.ascontiguousarray(a)
    wkv = np.asarray(L0_xattn_Wkv)
    wk = wkv[:, :INNER].reshape(D, G, 2, 2, 2, DH // 2).transpose(0, 1, 4, 3, 2, 5).reshape(D, INNER)
    arrays = {
        "x": f(x),
        "ctx_in": f(ctx_1024),
        "cos_t": f(np.tile(np.asarray(L0_xattn_cos).T, (GH, 1))),
        "sin_t": f(np.tile(np.asarray(L0_xattn_sin).T, (GH, 1))),
        "vecs": f(np.stack([np.asarray(a) for a in (L0_xattn_ln_lat_g, L0_xattn_ln_lat_b, L0_xattn_ln_ctx_g,
                                                     L0_xattn_ln_ctx_b)], axis=1)),
        "wk": f(wk),
        "wq": f(np.asarray(L0_xattn_Wq).reshape(D, HEADS, 2, DH // 2).transpose(0, 1, 3, 2).reshape(D, INNER)),
        "wv": f(wkv[:, INNER:]),
        "wo": f(L0_xattn_Wo),
        "bo": f(L0_xattn_bo),
        "router_t": f(np.asarray(L0_ffn_router_w).T),
        "w1_t": f(np.asarray(L0_ffn_w1).transpose(2, 0, 1).reshape(D, E * FF)),
        "b1_t": f(np.asarray(L0_ffn_b1).reshape(FT, P).T),
        "w2_t": f(np.asarray(L0_ffn_w2).transpose(0, 2, 1).reshape(FT, P, D).transpose(1, 0, 2).reshape(P, FT * D)),
        "b2": f(L0_ffn_b2),
        "consts": constants(),
    }
    nc = bacc.Bacc("TRN2", target_bir_lowering=False, num_devices=1)
    args = {n: nc.dram_tensor(n, a.shape, mybir.dt.from_np(a.dtype), kind="ExternalInput").ap()
            for n, a in arrays.items()}
    args["out"] = nc.dram_tensor("out", (B, NQ, D), F32, kind="ExternalOutput").ap()
    build(nc, **args)
    r = run_bass_kernel_spmd(nc, [arrays], core_ids=[0])
    return r.results[0]["out"]
```

```python
from contextlib import ExitStack

import numpy as np

import concourse.bass as bass
from concourse import mybir

F32 = mybir.dt.float32
F32R = mybir.dt.float32r
U32 = mybir.dt.uint32
ALU = mybir.AluOpType
ACT = mybir.ActivationFunctionType

P = 128
B = 4
NQ = 256
NK = 512
D = 128
HEADS = 16
DH = 64
INNER = HEADS * DH
G = 4
GH = HEADS // G
PAIRS = HEADS // 2
KT = NK // P
QT = NQ // P
TOK = B * NQ
TT = TOK // P
E = 8
FF = 256
FT = E * FF // P
CH = 512
CHUNKS = TOK // CH
EPS = 1e-5
CLIP = 11.0
E_MIN = float(np.exp(np.float32(-CLIP)))
E_MAX = float(np.exp(np.float32(CLIP)))
SCALE = DH ** -0.5

WK_HI, WK_LO, WQ_HI, WQ_LO, WV_HI, WV_LO = (INNER * n for n in range(6))
W1_HI, W1_LO, W2_HI, W2_LO = (E * FF * n for n in range(4))

C_ID = 0
C_SEL = C_ID + P
C_HEAD = C_SEL + G * 32
C_EXP = C_HEAD + PAIRS * P
C_IOTA = C_EXP + E * P
C_ALL = C_IOTA + TT * E


def constants():
    c = np.zeros((P, C_ALL), np.float32)
    c[:, C_ID:C_ID + P] = np.eye(P, dtype=np.float32)
    for g in range(G):
        c[:, C_SEL + 32 * g + g] = 1
    c[:, C_SEL + G:C_SEL + 32] = 1
    for h in range(HEADS):
        row, at = 32 * (h % GH) + h // GH, C_HEAD + (h // 2) * P + (h % 2) * DH
        c[row, at:at + DH] = 1
    for e in range(E):
        c[e, C_EXP + e * P:C_EXP + (e + 1) * P] = 1
        c[E + e, C_EXP + e * P:C_EXP + (e + 1) * P] = 1
    c[:, C_IOTA:] = np.tile(np.arange(E, dtype=np.float32), TT)
    return c


class Chain:

    def __init__(self, eng, sem, per_round):
        self.eng, self.sem, self.per, self.n, self.base = eng, sem, per_round, 0, 0

    def start(self, round_):
        self.base, self.n = round_ * self.per, 0

    def put(self, ins):
        self.n += 1
        ins.then_inc(self.sem, 1)

    def wait(self):
        self.eng.wait_ge(self.sem, self.base + self.n)

    def link(self, ins):
        self.put(ins)
        self.wait()

    def end(self):
        assert self.n == self.per, (self.n, self.per)


def after(eng, sem, count):
    if not isinstance(count, int) or count > 0:
        eng.wait_ge(sem, count)


REST = 9
ATTN = 3
AHEAD = 3
LAG = 4
BUF = 4
X_AT = B * KT
X2_AT = X_AT + TT
SLOTS = X2_AT + TT
ROUTES = ((0, TT - QT), (TT - QT, TT))


def build(nc, x, ctx_in, cos_t, sin_t, vecs, wk, wq, wv, wo, bo, router_t, w1_t, b1_t, w2_t, b2, consts, out):
    stack = ExitStack()
    k_scratch = nc.dram_tensor("k_scratch", [G, GH, P, NK], F32, kind="Internal").ap()
    q_scratch = nc.dram_tensor("q_scratch", [G, GH, DH, NQ], F32, kind="Internal").ap()
    with stack:
        def sb(name, shape, dt=F32):
            return stack.enter_context(nc.sbuf_tensor(name, shape, dt))

        def sem(name):
            return stack.enter_context(nc.semaphore(name))

        def flat(ap):
            return ap.rearrange("p a b -> p (a b)")

        w_split = sb("w_split", [P, 4 * E * FF], F32R)
        wo_sb = sb("wo_sb", [P, PAIRS, D])
        k_stack = sb("k_stack", [P, HEADS, NK], F32R)
        q_dup = sb("q_dup", [P, HEADS, NQ], F32R)
        q_lo = sb("q_lo", [P, PAIRS, NQ], F32R)
        v_sb = sb("v_sb", [P, KT, INNER])
        e_raw = sb("e_raw", [P, 2, KT * NQ])
        e_clip = sb("e_clip", [P, 4, KT * NQ])
        half_sum = sb("half_sum", [P, 2 * NQ])
        key_sum = sb("key_sum", [P, 8, NQ])
        rope_c = sb("rope_c", [P, 2, NK])
        rope_s = sb("rope_s", [P, 2, NK])
        k_hi = sb("k_hi", [P, 2, NK], F32R)
        k_lo = sb("k_lo", [P, 2, NK], F32R)
        q_hi = sb("q_hi", [P, 2, NQ], F32R)
        cT_all = sb("cT_all", [P, B, NK])
        xT_all = sb("xT_all", [P, B, NQ])
        cT_hi = sb("cT_hi", [P, NK], F32R)
        cT_lo = sb("cT_lo", [P, NK], F32R)
        xT_hi = sb("xT_hi", [P, NQ], F32R)
        xT_lo = sb("xT_lo", [P, NQ], F32R)
        o_sb = sb("o_sb", [P, PAIRS, NQ])
        recip = sb("recip", [P, NQ])
        recip_hi = sb("recip_hi", [P, NQ], F32R)
        recip_lo = sb("recip_lo", [P, NQ], F32R)
        x_all = sb("x_all", [P, TT, D])
        cos_sb = sb("cos_sb", [P, NK])
        sin_sb = sb("sin_sb", [P, NK])
        bo_sb = sb("bo_sb", [P, D])
        vec_sb = sb("vec_sb", [P, 4])
        b1_sb = sb("b1_sb", [P, FT])
        router_sb = sb("router_sb", [P, E])
        b2_sb = sb("b2_sb", [2 * E, D])
        ident = sb("ident", [P, P])
        sel_sum = sb("sel_sum", [P, G, 32])
        sel_head = sb("sel_head", [P, PAIRS, P], F32R)
        iota = sb("iota", [P, TT, E])
        stats = sb("stats", [P, SLOTS, 6])
        mv = sb("mv", [P, SLOTS, 2])
        var_eps = sb("var_eps", [P, SLOTS])
        rstd = sb("rstd", [P, SLOTS])
        minus_half = sb("minus_half", [P, SLOTS])
        euler = sb("euler", [P, TT])
        logits = sb("logits", [P, TT, E])
        max8 = sb("max8", [P, TT, E])
        idx8 = sb("idx8", [P, TT, E], U32)
        idx_f = sb("idx_f", [P, TT, 2])
        top = sb("top", [P, 5, TT])
        one1 = sb("one1", [P, TT, E])
        one2 = sb("one2", [P, TT, E])
        comb = sb("comb", [P, TT, 2 * E])
        w_raw = e_clip
        head_raw = flat(rope_c[:])
        c_rows = e_raw[:].rearrange("p a (t d) -> p (a t) d", d=D)
        x_rows = key_sum[:, 0:4, :].rearrange("p a (t d) -> p (a t) d", d=D)
        w1_raw = flat(cT_all[:])
        w2_raw = (flat(rope_c[:]), flat(rope_s[:]))
        exp_raw = flat(k_lo[:])[0:2 * E, :].bitcast(F32)
        h_norm = flat(k_hi[:]).bitcast(F32).rearrange("p (t d) -> p t d", d=D)
        hT = flat(xT_all[:])
        hT_hi = flat(q_dup[:, 0:4, :])
        hT_lo = flat(q_dup[:, 4:8, :])
        combT = flat(k_stack[0:2 * E, 0:2, :])
        sel_exp = flat(k_stack[0:2 * E, 2:4, :])
        b2_hi = q_dup[0:2 * E, 8, 0:D]
        b2_lo = q_dup[0:2 * E, 8, D:2 * D]
        mid_hi = k_stack[:, 4:4 + BUF, :]
        mid_lo = k_stack[:, 8:8 + BUF, :]
        act_out = v_sb[:, 0:2, :].rearrange("p a (b n) -> p (a b) n", n=CH)
        mid = v_sb[:, 2:4, :].rearrange("p a (b n) -> p (a b) n", n=CH)
        yT = e_raw[:, 0, 0:CH]
        y_out = e_raw[:, 1, 0:CH].rearrange("p (t d) -> p t d", d=D)

        ps = [stack.enter_context(nc.psum_tensor(f"ps{n}", [P, 2, 512], F32)) for n in range(4)]

        def bank(n):
            return ps[n // 2][:, n % 2, :]

        KEY_B, QUERY_B, VALUE_B = 3, 6, (7, 6)
        AHEAD_B = ((3, 4, (5, 7)), (0, 4, (5, 6)), (1, 4, (5, 7)))
        SPREAD_B, SPREAD_LAST_B, OUT_B = (5, 7, 4, 5), (5, 7, 6, 5), 5
        COMB_B, UP_B, RESULT_B, TURNED_B = (1, 4), (2, 3), (0, 5), 7

        in_first = sem("in_first")
        in_qkv = [sem(f"in_qkv{n}") for n in range(3)]
        in_rope = sem("in_rope")
        in_more = sem("in_more")
        in_rest = sem("in_rest")
        in_up = sem("in_up")
        in_down = sem("in_down")
        in_exp = sem("in_exp")
        w_hi_done = sem("w_hi_done")
        w_lo_done = sem("w_lo_done")
        sel_done = sem("sel_done")
        const_done = sem("const_done")
        dve_pro = sem("dve_pro")
        dve_split = sem("dve_split")
        dve_rope = sem("dve_rope")
        var_done = sem("var_done")
        rstd_done = sem("rstd_done")
        norm0_done = sem("norm0_done")
        pool_pro = sem("pool_pro")
        x1_done = sem("x1_done")
        more_done = sem("more_done")
        turned0 = sem("turned0")
        turned = sem("turned")
        affine0 = sem("affine0")
        affine0x = sem("affine0x")
        affine = sem("affine")
        c_hi_done = sem("c_hi_done")
        split_done = sem("split_done")
        k_filled = sem("k_filled")
        k_taken = sem("k_taken")
        rope_done = sem("rope_done")
        k_hi_done = sem("k_hi_done")
        k_lo_done = sem("k_lo_done")
        k_stored = sem("k_stored")
        k_loaded = [sem(f"k_loaded{g}") for g in range(G)]
        q_filled = sem("q_filled")
        q_hi_done = sem("q_hi_done")
        q_lo_done = sem("q_lo_done")
        q_stored = sem("q_stored")
        q_loaded = [sem(f"q_loaded{g}") for g in range(G)]
        v_filled = sem("v_filled")
        v_done = sem("v_done")
        scores_done = sem("scores_done")
        exp_done = sem("exp_done")
        clip_done = sem("clip_done")
        half_done = sem("half_done")
        ksum_done = sem("ksum_done")
        pv_done = sem("pv_done")
        pv_taken = sem("pv_taken")
        sums_done = sem("sums_done")
        dve_attn = sem("dve_attn")
        recip_done = sem("recip_done")
        spread_done = sem("spread_done")
        scaled_done = sem("scaled_done")
        y_done = sem("y_done")
        resid_done = sem("resid_done")
        dve_route = sem("dve_route")
        rvar_done = sem("rvar_done")
        rrstd_done = sem("rrstd_done")
        hn_done = sem("hn_done")
        hT_filled = sem("hT_filled")
        hT_done = sem("hT_done")
        hT_hi_done = sem("hT_hi_done")
        hT_lo_done = sem("hT_lo_done")
        logits_done = sem("logits_done")
        gap_done = sem("gap_done")
        gap_exp = sem("gap_exp")
        comb_done = sem("comb_done")
        combT_filled = sem("combT_filled")
        combT_done = sem("combT_done")
        b2_done = sem("b2_done")
        w12_hi_done = sem("w12_hi_done")
        w12_lo_done = sem("w12_lo_done")
        cb_filled = sem("cb_filled")
        up_done = sem("up_done")
        gelu_done = sem("gelu_done")
        mid_done = sem("mid_done")
        mid_hi_done = sem("mid_hi_done")
        mid_lo_done = sem("mid_lo_done")
        down_done = sem("down_done")
        yT_done = sem("yT_done")
        yTT_done = sem("yTT_done")
        final_done = sem("final_done")
        stored = sem("stored")

        block = stack.enter_context(nc.Block())


        @block.sync
        def _(sp):
            sp.dma_start(c_rows[:, 0:KT, :], ctx_in[0].rearrange("(t p) d -> p t d", p=P)).then_inc(in_first, 16)
            sp.dma_start(x_all[:, 0:QT, :], x[0].rearrange("(t p) d -> p t d", p=P)).then_inc(in_first, 16)
            sp.dma_start(w_raw[:, 0, :], wk).then_inc(in_qkv[0], 16)
            sp.dma_start(ident[:], consts[:, C_ID:C_ID + P]).then_inc(in_first, 16)
            sp.dma_start(vec_sb[:], vecs).then_inc(in_first, 16)
            sp.dma_start(w_raw[:, 1, :], wq).then_inc(in_qkv[1], 16)
            sp.dma_start(cos_sb[:], cos_t).then_inc(in_rope, 16)
            sp.dma_start(sin_sb[:], sin_t).then_inc(in_rope, 16)
            sp.dma_start(w_raw[:, 2, :], wv).then_inc(in_qkv[2], 16)
            sp.dma_start(c_rows[:, KT:, :], ctx_in[1:].rearrange("b (t p) d -> p (b t) d", p=P)).then_inc(in_more, 16)
            sp.dma_start(x_all[:, QT:, :], x[1:].rearrange("b (t p) d -> p (b t) d", p=P)).then_inc(in_more, 16)
            rest = [
                (head_raw, consts[:, C_HEAD:C_HEAD + PAIRS * P]),
                (sel_sum[:].rearrange("p g m -> p (g m)"), consts[:, C_SEL:C_SEL + G * 32]),
                (wo_sb[:], wo.rearrange("(c p) n -> p c n", p=P)),
                (bo_sb[:], bo.partition_broadcast(P)),
                (iota[:].rearrange("p t e -> p (t e)"), consts[:, C_IOTA:C_IOTA + TT * E]),
                (b1_sb[:], b1_t), (router_sb[:], router_t), (b2_sb[0:E, :], b2), (b2_sb[E:2 * E, :], b2),
            ]
            for dst, src in rest:
                sp.dma_start(dst, src).then_inc(in_rest, 16)
            assert len(rest) == REST

            def move_group(n, g):
                sp.wait_ge(q_hi_done, n + 1)
                sp.dma_start(q_scratch[g].rearrange("(a h) d q -> (h d) a q", a=2),
                             q_hi[:].bitcast(F32)).then_inc(q_stored, 16)
                for part, hi, ready in ((k_hi, True, k_hi_done), (k_lo, False, k_lo_done)):
                    sp.wait_ge(ready, n + 1)
                    for odd in range(2):
                        at = 0 if hi != bool(odd) else DH
                        dst = k_scratch[g].rearrange("(jj jo) r s -> jo jj r s", jo=2)[odd, :, at:at + DH, :]
                        sp.dma_start(dst.rearrange("jj (r x) s -> jj r (x s)", x=2),
                                     flat(part[DH * odd:DH * odd + DH, :, :]).bitcast(F32)).then_inc(k_stored, 16)
                heads = slice(g * GH, (g + 1) * GH)
                sp.wait_ge(k_stored, (n + 1) * 64)
                sp.dma_start(k_stack[:, heads, :].bitcast(F32),
                             k_scratch[g].rearrange("h r s -> r h s")).then_inc(k_loaded[g], 16)
                sp.wait_ge(q_stored, (n + 1) * 16)
                for side in range(2):
                    sp.dma_start(q_dup[DH * side:DH * side + DH, heads, :].bitcast(F32),
                                 q_scratch[g].rearrange("h d q -> d h q")).then_inc(q_loaded[g], 16)

            for n in range(AHEAD):
                move_group(n, n)
            with sp.Fori(0, B - 1) as b:
                for s in range(G):
                    move_group(b * G + AHEAD + s, (AHEAD + s) % G)
            sp.wait_ge(split_done, B)
            sp.wait_ge(c_hi_done, B)
            sp.dma_start(w1_raw, w1_t).then_inc(in_up, 16)
            move_group(B * G - 1, G - 1)
            for n in range(2):
                sp.dma_start(w2_raw[n], w2_t[:, n * 2 * NK:(n + 1) * 2 * NK]).then_inc(in_down, 16)
            sp.dma_start(exp_raw, consts[0:2 * E, C_EXP:C_EXP + E * P]).then_inc(in_exp, 16)
            for c in range(CHUNKS):
                sp.wait_ge(final_done, c + 1)
                sp.dma_start(out[c * CH // NQ:(c + 1) * CH // NQ].rearrange("b (t p) d -> p (b t) d", p=P),
                             y_out).then_inc(stored, 16)
            sp.wait_ge(stored, 16 * CHUNKS)

        @block.tensor
        def _(pe):
            mm = nc.tensor.matmul

            def three(dst, w, w_lo, m, m_lo, start=True, stop=True):
                mm(dst, w, m, start=start, stop=False)
                mm(dst, w_lo, m, start=False, stop=False)
                return mm(dst, w, m_lo, start=False, stop=stop)

            def turn(dst, rows):
                for t, row in enumerate(rows):
                    ins = nc.tensor.transpose(dst[:, t * P:(t + 1) * P], row, ident[:])
                return ins

            def keys(n, g, pair=KEY_B):
                if g == 0:
                    pe.wait_ge(split_done, nb_of(n) + 1)
                after(pe, v_done, 2 * n if pair == KEY_B else 0)
                for half in range(2):
                    at = (2 * g + half) * P
                    ins = three(ps[pair][:, half, :], w_split[:, WK_HI + at:WK_HI + at + P],
                                w_split[:, WK_LO + at:WK_LO + at + P], cT_hi[:], cT_lo[:])
                ins.then_inc(k_filled, 1)

            def queries(n, g, to=QUERY_B):
                for pair in range(2):
                    at = (2 * g + pair) * P
                    ins = three(bank(to)[:, pair * NQ:(pair + 1) * NQ], w_split[:, WQ_HI + at:WQ_HI + at + P],
                                w_split[:, WQ_LO + at:WQ_LO + at + P], xT_hi[:], xT_lo[:])
                ins.then_inc(q_filled, 1)

            def values(n, g, half, to=None):
                to = VALUE_B[half] if to is None else to
                w = GH * DH
                for t in range(2):
                    kt = 2 * half + t
                    ins = three(bank(to)[:, t * w:(t + 1) * w], cT_hi[:, kt * P:(kt + 1) * P],
                                cT_lo[:, kt * P:(kt + 1) * P], w_split[:, WV_HI + g * w:WV_HI + (g + 1) * w],
                                w_split[:, WV_LO + g * w:WV_LO + (g + 1) * w])
                ins.then_inc(v_filled, 1)

            def nb_of(n):
                return n // G if isinstance(n, int) else open_batch[0]

            open_batch = [None]

            def scores(b, h):
                g, odd = h // GH, h % 2
                if h % GH == 0:
                    pe.wait_ge(k_loaded[g], b * 16 + 16)
                    pe.wait_ge(q_loaded[g], b * 32 + 32)
                    pe.wait_ge(q_lo_done, b * G + g + 1)
                after(pe, exp_done, b * HEADS + h - 1)
                hi_rows = slice(DH * odd, DH * odd + DH)
                for kt in range(KT):
                    dst = ps[h % 2][:, kt // 2, (kt % 2) * NQ:(kt % 2) * NQ + NQ]
                    keys_ = slice(kt * P, (kt + 1) * P)
                    mm(dst, k_stack[:, h, keys_], q_dup[:, h, :], start=True, stop=False)
                    ins = mm(dst, k_stack[hi_rows, h, keys_], q_lo[hi_rows, h // 2, :], start=False, stop=True)
                ins.then_inc(scores_done, 1)

            def weigh(b, pair):
                if pair % 2 == 0:
                    pe.wait_ge(v_done, b * 2 * G + pair + 2)
                pe.wait_ge(clip_done, b * HEADS + 2 * pair + 2)
                after(pe, pv_taken, b * PAIRS + pair)
                for kt in range(KT):
                    for odd in range(2):
                        h = 2 * pair + odd
                        ins = mm(bank(4)[DH * odd:DH * odd + DH, 0:NQ], v_sb[:, kt, h * DH:(h + 1) * DH],
                                 e_clip[:, h % 4, kt * NQ:(kt + 1) * NQ], start=(kt == 0), stop=(kt == KT - 1))
                ins.then_inc(pv_done, 1)

            def sums(b, g):
                pe.wait_ge(ksum_done, b * HEADS + (g + 1) * GH)
                if g == 0:
                    after(pe, resid_done, b)
                for j in range(GH):
                    ins = mm(bank(5)[32 * j:32 * j + 32, 0:NQ], sel_sum[:, g, :], key_sum[:, (g * GH + j) % 8, :],
                             start=(g == 0), stop=(g == G - 1))
                ins.then_inc(sums_done, 1)

            def spread(b, k, banks):
                if k == 0:
                    pe.wait_ge(recip_done, b + 1)
                if k == 2:
                    pe.wait_ge(pv_taken, b * PAIRS + PAIRS)
                if k == 3:
                    pe.wait_ge(scaled_done, b * 4 + 1)
                for pair in (2 * k, 2 * k + 1):
                    dst = bank(banks[k])[:, (pair % 2) * NQ:(pair % 2) * NQ + NQ]
                    mm(dst, sel_head[:, pair, :], recip_hi[:], start=True, stop=False)
                    ins = mm(dst, sel_head[:, pair, :], recip_lo[:], start=False, stop=True)
                ins.then_inc(spread_done, 1)

            def project(b):
                pe.wait_ge(scaled_done, b * 4 + 4)
                for t in range(QT):
                    for pair in range(PAIRS):
                        ins = mm(bank(OUT_B)[:, t * D:(t + 1) * D], o_sb[:, pair, t * P:(t + 1) * P],
                                 wo_sb[:, pair, :], start=(pair == 0), stop=(pair == PAIRS - 1))
                ins.then_inc(y_done, 1)

            def route(r, part):
                t0, t1 = ROUTES[r]
                tiles = range(t0, t1)
                if part == 0:
                    pe.wait_ge(hn_done, r + 1)
                    after(pe, combT_done, r)
                    for i, t in enumerate(tiles):
                        ins = turn(bank(6 + i // 4)[:, (i % 4) * P:], [h_norm[:, t, :]])
                    ins.then_inc(hT_filled, 1)
                if part == 1:
                    pe.wait_ge(hT_done, r + 1)
                    for i, t in enumerate(tiles):
                        ins = mm(bank(6)[:, i * E:(i + 1) * E], hT[:, t * P:(t + 1) * P], router_sb[:],
                                 start=True, stop=True)
                    ins.then_inc(logits_done, 1)
                if part == 2:
                    pe.wait_ge(comb_done, r + 1)
                    for i, t in enumerate(tiles):
                        ins = turn(bank(6 + i // 4)[0:2 * E, (i % 4) * P:], [comb[:, t, :]])
                    ins.then_inc(combT_filled, 1)

            def batch(b, first=False, last=False):
                for p in range(PAIRS):
                    s, even = p // 2, p % 2 == 0
                    fill = not last or s == 0
                    n, g = b * G + AHEAD + s, (AHEAD + s) % G
                    open_batch[0] = b + 1
                    scores(b, 2 * p)
                    scores(b, 2 * p + 1)
                    if fill and even:
                        keys(n, g)
                    if p == 0 and not first:
                        weigh(b - 1, PAIRS - 1)
                        sums(b - 1, G - 1)
                    if p == 1 and not first:
                        for k in range(4):
                            spread(b - 1, k, SPREAD_B)
                        project(b - 1)
                    if fill and not even:
                        pe.wait_ge(k_taken, n + 1)
                        values(n, g, 0)
                    if p >= 1:
                        weigh(b, p - 1)
                    if not even and p >= 3:
                        sums(b, (p - 3) // 2)
                    if fill and even:
                        pe.wait_ge(k_taken, n + 1)
                        queries(n, g)
                    if fill and not even:
                        pe.wait_ge(q_lo_done, n + 1)
                        values(n, g, 1)
                    if last and p == 3:
                        route(0, 0)
                    if last and p == 4:
                        route(0, 1)
                    if last and p == 6:
                        route(0, 2)

            pe.wait_ge(in_first, 64)
            pe.wait_ge(norm0_done, 1)
            turn(bank(0), [c_rows[:, t, :] for t in range(KT)]).then_inc(turned0, 1)
            pe.wait_ge(norm0_done, 2)
            turn(bank(1), [x_rows[:, t, :] for t in range(QT)]).then_inc(turned0, 1)
            for n, (pair, q_bank, v_banks) in enumerate(AHEAD_B):
                if n == 0:
                    pe.wait_ge(w_lo_done, 1)
                keys(n, n, pair)
            for n, (pair, q_bank, v_banks) in enumerate(AHEAD_B):
                if n == 0:
                    pe.wait_ge(w_lo_done, 3)
                after(pe, q_lo_done, n)
                queries(n, n, q_bank)
                after(pe, v_done, 2 * n - 1)
                values(n, n, 0, v_banks[0])
                pe.wait_ge(k_taken, 1 if n < 2 else 0) if n < 2 else pe.wait_ge(v_done, 2)
                values(n, n, 1, v_banks[1])
            pe.wait_ge(more_done, 1)
            pe.wait_ge(k_taken, AHEAD)
            for i in range(1, B):
                turn(bank(i - 1), [c_rows[:, i * KT + t, :] for t in range(KT)]).then_inc(turned, 1)
            turn(bank(3), [x_rows[:, QT + t, :] for t in range(4)]).then_inc(turned, 1)
            pe.wait_ge(v_done, 2 * AHEAD - 1)
            turn(bank(5), [x_rows[:, QT + 4 + t, :] for t in range(2)]).then_inc(turned, 1)
            pe.wait_ge(affine, 5)
            pe.wait_ge(in_rest, REST * 16)
            pe.wait_ge(sel_done, 1)

            batch(0, first=True)
            with pe.Fori(1, B - 1) as b:
                batch(b)
            batch(B - 1, last=True)
            weigh(B - 1, PAIRS - 1)
            sums(B - 1, G - 1)

            pe.wait_ge(hT_lo_done, 1)
            pe.wait_ge(hT_hi_done, 1)
            pe.wait_ge(combT_done, 1)
            pe.wait_ge(w12_hi_done, 2)
            pe.wait_ge(w12_lo_done, 2)
            pe.wait_ge(b2_done, 1)
            pe.wait_ge(exp_done, B * HEADS)
            pe.wait_ge(pv_taken, B * PAIRS)
            for c in range(CHUNKS):
                tok = slice(c * CH, (c + 1) * CH)
                result = bank(RESULT_B[c])

                def up(f):
                    n, e = c * FT + f, f // 2
                    if f % 2 == 0:
                        after(pe, mid_done, 2 * (c * E + e - 1))
                        mm(bank(COMB_B[e % 2]), sel_exp[:, e * P:(e + 1) * P], combT[:, tok],
                           start=True, stop=True).then_inc(cb_filled, 1)
                    after(pe, gelu_done, n - 1)
                    three(bank(UP_B[f % 2]), w_split[:, W1_HI + f * P:W1_HI + (f + 1) * P],
                          w_split[:, W1_LO + f * P:W1_LO + (f + 1) * P],
                          hT_hi[:, tok], hT_lo[:, tok]).then_inc(up_done, 1)

                def down(f):
                    n = c * FT + f
                    pe.wait_ge(mid_lo_done, n + 1)
                    three(result, w_split[:, W2_HI + f * P:W2_HI + (f + 1) * P],
                          w_split[:, W2_LO + f * P:W2_LO + (f + 1) * P], mid_hi[:, f % BUF, :],
                          mid_lo[:, f % BUF, :], start=False, stop=(f == FT - 1)).then_inc(down_done, 1)

                if c:
                    pe.wait_ge(hT_lo_done, 2)
                    pe.wait_ge(hT_hi_done, 2)
                    pe.wait_ge(combT_done, 2)
                mm(result, b2_hi, combT[:, tok], start=True, stop=False)
                mm(result, b2_lo, combT[:, tok], start=False, stop=False)
                for f in range(FT + LAG):
                    if f < FT:
                        up(f)
                    if f >= LAG:
                        down(f - LAG)
                    if c == 0 and f == 1:
                        for k in range(4):
                            spread(B - 1, k, SPREAD_LAST_B)
                    if c == 0 and f == 2:
                        project(B - 1)
                    if c == 0 and f in ROUTE_AT:
                        route(1, ROUTE_AT.index(f))
                    if c == 1 and f == 1:
                        pe.wait_ge(yT_done, 1)
                        turn(bank(TURNED_B), [yT[:, t * P:(t + 1) * P] for t in range(4)]).then_inc(yTT_done, 1)
            pe.wait_ge(yT_done, CHUNKS)
            pe.wait_ge(final_done, CHUNKS - 1)
            turn(bank(TURNED_B), [yT[:, t * P:(t + 1) * P] for t in range(4)]).then_inc(yTT_done, 1)

        @block.scalar
        def _(act):
            copy = nc.scalar.copy

            def affine_rows(dst, src, gain):
                return nc.scalar.activation(dst, src, ACT.Identity, bias=vec_sb[:, gain + 1:gain + 2],
                                            scale=vec_sb[:, gain:gain + 1])

            def context_hi(nb):
                after(act, v_filled, nb * 2 * G)
                copy(cT_hi[:], cT_all[:, bass.ds(nb, 1), :].rearrange("p a k -> p (a k)")).then_inc(c_hi_done, 1)

            def keys_hi(n):
                act.wait_ge(rope_done, n + 1)
                after(act, k_stored, n * 64)
                copy(flat(k_hi[:]), flat(rope_c[:])).then_inc(k_hi_done, 1)

            def queries_hi(n, at=QUERY_B):
                act.wait_ge(q_filled, n + 1)
                after(act, q_stored, n * 16)
                copy(flat(q_hi[:]), bank(at)).then_inc(q_hi_done, 1)

            def values_out(n, g, half, at=None):
                at = VALUE_B[half] if at is None else at
                w = GH * DH
                act.wait_ge(v_filled, 2 * n + half + 1)
                copy(v_sb[:, 2 * half:2 * half + 2, g * w:(g + 1) * w],
                     bank(at).rearrange("p (t n) -> p t n", t=2)).then_inc(v_done, 1)

            def exps(b, h):
                act.wait_ge(scores_done, b * HEADS + h + 1)
                after(act, clip_done, b * HEADS + h - 1)
                nc.scalar.activation(e_raw[:, h % 2, :], flat(ps[h % 2][:, :, :]), ACT.Exp,
                                     scale=SCALE).then_inc(exp_done, 1)

            def take(b, pair):
                act.wait_ge(pv_done, b * PAIRS + pair + 1)
                copy(o_sb[:, pair, :], bank(4)[:, 0:NQ]).then_inc(pv_taken, 1)

            def route(r, part):
                t0, t1 = ROUTES[r]
                cols = slice(t0 * P, t1 * P)
                if part == 1:
                    act.wait_ge(hT_done, r + 1)
                    copy(hT_hi[:, cols], hT[:, cols]).then_inc(hT_hi_done, 1)
                if part == 2:
                    act.wait_ge(combT_filled, r + 1)
                    w = (t1 - t0) * P
                    copy(combT[:, cols], flat(ps[3][0:2 * E, :, :])[:, 0:w]).then_inc(combT_done, 1)

            def batch(b, first=False, last=False):
                for p in range(PAIRS):
                    s, even = p // 2, p % 2 == 0
                    fill = not last or s == 0
                    n, g = b * G + AHEAD + s, (AHEAD + s) % G
                    if p == 2 and not last:
                        context_hi(b + 1)
                    exps(b, 2 * p)
                    exps(b, 2 * p + 1)
                    if fill and not even:
                        values_out(n, g, 0)
                    if p == 0 and not first:
                        take(b - 1, PAIRS - 1)
                    if p >= 1:
                        take(b, p - 1)
                    if fill and even:
                        keys_hi(n)
                        queries_hi(n)
                    if fill and not even:
                        values_out(n, g, 1)
                    if last and p == 3:
                        act.wait_ge(in_up, 16)
                        copy(w_split[:, W1_HI:W1_HI + E * FF], w1_raw).then_inc(w12_hi_done, 1)
                    if last and p == 4:
                        act.wait_ge(in_down, 32)
                        for i in range(2):
                            at = W2_HI + i * 2 * NK
                            ins = copy(w_split[:, at:at + 2 * NK], w2_raw[i])
                        ins.then_inc(w12_hi_done, 1)
                        route(0, 1)
                    if last and p == 6:
                        route(0, 2)

            for i, at in enumerate((WK_HI, WQ_HI, WV_HI)):
                act.wait_ge(in_qkv[i], 16)
                copy(w_split[:, at:at + INNER], w_raw[:, i, :]).then_inc(w_hi_done, 1)
            act.wait_ge(in_first, 64)
            act.wait_ge(turned0, 1)
            affine_rows(cT_all[:, 0, :], bank(0), 2).then_inc(affine0, 1)
            act.wait_ge(affine0, 1)
            context_hi(0)
            for n, (pair, q_bank, v_banks) in enumerate(AHEAD_B):
                if n == 0:
                    queries_hi(n, q_bank)
                    values_out(n, n, 0, v_banks[0])
                    keys_hi(n)
                else:
                    keys_hi(n)
                    queries_hi(n, q_bank)
                    values_out(n, n, 0, v_banks[0])
                values_out(n, n, 1, v_banks[1])
            for i in range(1, B):
                act.wait_ge(turned, i)
                affine_rows(cT_all[:, i, :], bank(i - 1), 2).then_inc(affine, 1)
            act.wait_ge(turned, B)
            affine_rows(flat(xT_all[:, 1:3, :]), bank(3), 0).then_inc(affine, 1)
            act.wait_ge(turned, B + 1)
            affine_rows(xT_all[:, 3, :], bank(5)[:, 0:NQ], 0).then_inc(affine, 1)

            batch(0, first=True)
            with act.Fori(1, B - 1) as b:
                batch(b)
            batch(B - 1, last=True)
            take(B - 1, PAIRS - 1)

            for c in range(CHUNKS):
                def gelu(f):
                    n = c * FT + f
                    act.wait_ge(up_done, n + 1)
                    after(act, mid_done, n - BUF + 1)
                    nc.scalar.activation(act_out[:, f % BUF, :], bank(UP_B[f % 2]), ACT.Gelu,
                                         bias=b1_sb[:, f:f + 1]).then_inc(gelu_done, 1)

                def part(f):
                    n = c * FT + f
                    act.wait_ge(mid_done, n + 1)
                    after(act, down_done, n - BUF + 1)
                    copy(mid_hi[:, f % BUF, :], mid[:, f % BUF, :]).then_inc(mid_hi_done, 1)

                for f in range(FT + 1):
                    if f < FT:
                        gelu(f)
                    if f >= 1:
                        part(f - 1)
                    if c == 0 and f == ROUTE_AT[0]:
                        route(1, 1)
                    if c == 0 and f == ROUTE_AT[2]:
                        route(1, 2)
                act.wait_ge(down_done, (c + 1) * FT)
                after(act, yTT_done, c)
                copy(yT, bank(RESULT_B[c])).then_inc(yT_done, 1)

        @block.vector
        def _(dve):
            v = nc.vector
            pro = Chain(dve, dve_pro, 0)
            attn = Chain(dve, dve_attn, ATTN)
            rt = Chain(dve, dve_route, 0)

            def norm_stats(chain, rows, at):
                n = len(rows)
                for t in range(n):
                    chain.put(v.bn_stats(stats[:, at + t, :], rows[t]))
                chain.wait()
                for t in range(n):
                    chain.put(v.bn_aggr(mv[:, at + t, :], stats[:, at + t, :]))
                chain.wait()
                return v.tensor_scalar(var_eps[:, at:at + n], mv[:, at:at + n, 1], EPS, None, ALU.add)

            def normalise(dst, src, t):
                return v.tensor_scalar(dst, src, mv[:, t, 0:1], rstd[:, t:t + 1], ALU.subtract, ALU.mult)

            def split(nb):
                after(dve, v_filled, nb * 2 * G)
                xs = xT_all[:, bass.ds(nb, 1), :].rearrange("p a k -> p (a k)")
                cs = cT_all[:, bass.ds(nb, 1), :].rearrange("p a k -> p (a k)")
                v.tensor_copy(xT_hi[:], xs).then_inc(dve_split, 1)
                dve.wait_ge(c_hi_done, nb + 1)
                v.tensor_tensor(cT_lo[:], cs, cT_hi[:].bitcast(F32), ALU.subtract)
                dve.wait_ge(dve_split, nb + 1)
                v.tensor_tensor(xT_lo[:], xs, xT_hi[:].bitcast(F32), ALU.subtract).then_inc(split_done, 1)

            def rotate(n, pair=KEY_B):
                dve.wait_ge(k_filled, n + 1)
                after(dve, k_hi_done, n)
                after(dve, k_lo_done, n)
                both = ps[pair][:, :, :]
                v.tensor_tensor(rope_c[:], both, cos_sb[:].unsqueeze(1).to_broadcast([P, 2, NK]),
                                ALU.mult).then_inc(dve_rope, 1)
                v.tensor_tensor(rope_s[:], both, sin_sb[:].unsqueeze(1).to_broadcast([P, 2, NK]),
                                ALU.mult).then_inc(k_taken, 1)

            def rotate_sum(n):
                dve.wait_ge(dve_rope, 2 * n + 1)
                dve.wait_ge(k_taken, n + 1)
                v.tensor_tensor(rope_c[:, 0, :], rope_c[:, 0, :], rope_s[:, 1, :], ALU.subtract).then_inc(dve_rope, 1)
                v.tensor_tensor(rope_c[:, 1, :], rope_c[:, 1, :], rope_s[:, 0, :], ALU.add).then_inc(rope_done, 1)

            def keys_lo(n):
                dve.wait_ge(k_hi_done, n + 1)
                dve.wait_ge(rope_done, n + 1)
                after(dve, k_stored, n * 64)
                v.tensor_tensor(flat(k_lo[:]), flat(rope_c[:]), flat(k_hi[:]).bitcast(F32),
                                ALU.subtract).then_inc(k_lo_done, 1)

            def queries_lo(n, g, at=QUERY_B):
                dve.wait_ge(q_hi_done, n + 1)
                v.tensor_tensor(flat(q_lo[:, 2 * g:2 * g + 2, :]), bank(at), flat(q_hi[:]).bitcast(F32),
                                ALU.subtract).then_inc(q_lo_done, 1)

            def clip(b, h):
                dve.wait_ge(exp_done, b * HEADS + h + 1)
                after(dve, pv_done, b * PAIRS + h // 2 - 1)
                after(dve, ksum_done, b * HEADS + h - 3)
                v.tensor_scalar(e_clip[:, h % 4, :], e_raw[:, h % 2, :], E_MIN, E_MAX, ALU.max,
                                ALU.min).then_inc(clip_done, 1)

            def reciprocals(b):
                attn.start(b)
                dve.wait_ge(sums_done, b * G + G)
                attn.link(v.reciprocal(recip[:], bank(5)[:, 0:NQ]))
                attn.link(v.tensor_copy(recip_hi[:], recip[:]))
                v.tensor_tensor(recip_lo[:], recip[:], recip_hi[:].bitcast(F32), ALU.subtract).then_inc(recip_done, 1)

            def scale(b, k, banks):
                dve.wait_ge(spread_done, b * 4 + k + 1)
                dve.wait_ge(pv_taken, b * PAIRS + PAIRS)
                o = flat(o_sb[:, 2 * k:2 * k + 2, :])
                v.tensor_tensor(o, bank(banks[k]), o, ALU.mult).then_inc(scaled_done, 1)

            def residual(b):
                dve.wait_ge(y_done, b + 1)
                rows = x_all[:, bass.ds(b * QT, QT), :]
                attn.link(v.tensor_tensor(rows, bank(OUT_B)[:, 0:QT * D].rearrange("p (t d) -> p t d", t=QT), rows,
                                          ALU.add))
                v.tensor_tensor(rows, rows, bo_sb[:].unsqueeze(1).to_broadcast([P, QT, D]), ALU.add).then_inc(resid_done, 1)
                attn.end()

            def route(r, part):
                t0, t1 = ROUTES[r]
                n = t1 - t0
                tiles, cols = slice(t0, t1), slice(t0 * P, t1 * P)
                if part == 0:
                    dve.wait_ge(resid_done, B - 1 + r)
                    dve.wait_ge(k_stored, B * G * 64)
                    norm_stats(rt, [x_all[:, t, :] for t in range(t0, t1)], t0).then_inc(rvar_done, 1)
                    dve.wait_ge(rrstd_done, r + 1)
                    for t in range(t0, t1):
                        ins = normalise(h_norm[:, t, :], x_all[:, t, :], t)
                        if t < t1 - 1:
                            rt.put(ins)
                    ins.then_inc(hn_done, 1)
                if part == 1:
                    dve.wait_ge(hT_filled, r + 1)
                    v.tensor_copy(hT[:, cols], flat(ps[3][:, :, :])[:, 0:n * P]).then_inc(hT_done, 1)
                    dve.wait_ge(hT_hi_done, r + 1)
                    dve.wait_ge(hT_done, r + 1)
                    v.tensor_tensor(hT_lo[:, cols], hT[:, cols], hT_hi[:, cols].bitcast(F32),
                                    ALU.subtract).then_inc(hT_lo_done, 1)
                if part == 2:
                    dve.wait_ge(logits_done, r + 1)
                    rt.link(v.tensor_copy(logits[:, tiles, :].rearrange("p t e -> p (t e)"), bank(6)[:, 0:n * E]))
                    for t in range(t0, t1):
                        rt.put(v.max(max8[:, t, :], logits[:, t, :]))
                    rt.wait()
                    v.tensor_tensor(top[:, 0, tiles], max8[:, tiles, 1], max8[:, tiles, 0],
                                    ALU.subtract).then_inc(gap_done, 1)
                    for t in range(t0, t1):
                        rt.put(v.max_index(idx8[:, t, :], max8[:, t, :], logits[:, t, :]))
                    rt.wait()
                    rt.link(v.tensor_copy(idx_f[:, tiles, :], idx8[:, tiles, 0:2]))
                    for i, one in enumerate((one1, one2)):
                        rt.put(v.tensor_tensor(one[:, tiles, :], iota[:, tiles, :],
                                               idx_f[:, tiles, i:i + 1].to_broadcast([P, n, E]), ALU.is_equal))
                    dve.wait_ge(gap_exp, r + 1)
                    rt.link(v.tensor_scalar(top[:, 2, tiles], top[:, 1, tiles], 1.0, None, ALU.add))
                    rt.link(v.reciprocal(top[:, 3, tiles], top[:, 2, tiles]))
                    rt.link(v.tensor_tensor(top[:, 4, tiles], top[:, 1, tiles], top[:, 3, tiles], ALU.mult))
                    for i, one in enumerate((one1, one2)):
                        rt.put(v.tensor_tensor(one[:, tiles, :], one[:, tiles, :],
                                               top[:, 3 + i, tiles].unsqueeze(2).to_broadcast([P, n, E]), ALU.mult))
                    rt.wait()
                    rt.link(v.tensor_tensor(one1[:, tiles, :], one1[:, tiles, :], one2[:, tiles, :], ALU.add))
                    rt.link(v.tensor_copy(comb[:, tiles, 0:E].bitcast(F32R), one1[:, tiles, :]))
                    v.tensor_tensor(comb[:, tiles, E:2 * E], one1[:, tiles, :], comb[:, tiles, 0:E],
                                    ALU.subtract).then_inc(comb_done, 1)

            def batch(b, first=False, last=False):
                for p in range(PAIRS):
                    s, even = p // 2, p % 2 == 0
                    fill = not last or s == 0
                    n, g = b * G + AHEAD + s, (AHEAD + s) % G
                    if p == 2 and not last:
                        split(b + 1)
                    clip(b, 2 * p)
                    if fill and even:
                        rotate(n)
                    clip(b, 2 * p + 1)
                    if fill and even:
                        rotate_sum(n)
                    if p == 0 and not first:
                        reciprocals(b - 1)
                    if p == 1 and not first:
                        for k in range(4):
                            scale(b - 1, k, SPREAD_B)
                    if fill and not even:
                        keys_lo(n)
                        queries_lo(n, g)
                    if p == 1 and not first:
                        residual(b - 1)
                    if last and p == 2:
                        route(0, 0)
                    if last and p == 3:
                        dve.wait_ge(w12_hi_done, 1)
                        v.tensor_tensor(w_split[:, W1_LO:W1_LO + E * FF], w1_raw,
                                        w_split[:, W1_HI:W1_HI + E * FF].bitcast(F32), ALU.subtract).then_inc(w12_lo_done, 1)
                    if last and p == 4:
                        route(0, 1)
                    if last and p == 5:
                        dve.wait_ge(w12_hi_done, 2)
                        for i in range(2):
                            at = i * 2 * NK
                            ins = v.tensor_tensor(w_split[:, W2_LO + at:W2_LO + at + 2 * NK], w2_raw[i],
                                                  w_split[:, W2_HI + at:W2_HI + at + 2 * NK].bitcast(F32), ALU.subtract)
                        ins.then_inc(w12_lo_done, 1)
                        route(0, 2)
                    if last and p == 7:
                        dve.wait_ge(in_exp, 16)
                        rt.put(v.tensor_copy(sel_exp, exp_raw))
                        rt.link(v.tensor_copy(b2_hi, b2_sb[:]))
                        v.tensor_tensor(b2_lo, b2_sb[:], b2_hi.bitcast(F32), ALU.subtract).then_inc(b2_done, 1)

            def weight_lo(i):
                hi, lo = ((WK_HI, WK_LO), (WQ_HI, WQ_LO), (WV_HI, WV_LO))[i]
                dve.wait_ge(w_hi_done, i + 1)
                v.tensor_tensor(w_split[:, lo:lo + INNER], w_raw[:, i, :], w_split[:, hi:hi + INNER].bitcast(F32),
                                ALU.subtract).then_inc(w_lo_done, 1)

            dve.wait_ge(in_first, 64)
            norm_stats(pro, [x_all[:, t, :] for t in range(QT)], X_AT).then_inc(var_done, 1)
            norm_stats(pro, [c_rows[:, t, :] for t in range(KT)], 0).then_inc(var_done, 1)
            dve.wait_ge(rstd_done, 1)
            for t in range(QT):
                pro.put(normalise(x_rows[:, t, :], x_all[:, t, :], X_AT + t))
            pro.wait()
            norm_stats(pro, [x_rows[:, t, :] for t in range(QT)], X2_AT).then_inc(var_done, 1)
            dve.wait_ge(rstd_done, 2)
            for t in range(KT):
                ins = normalise(c_rows[:, t, :], c_rows[:, t, :], t)
                if t < KT - 1:
                    pro.put(ins)
            ins.then_inc(norm0_done, 1)
            weight_lo(0)
            dve.wait_ge(rstd_done, 3)
            for t in range(QT):
                ins = normalise(x_rows[:, t, :], x_rows[:, t, :], X2_AT + t)
                if t < QT - 1:
                    pro.put(ins)
            ins.then_inc(norm0_done, 1)
            dve.wait_ge(turned0, 2)
            v.tensor_scalar(xT_all[:, 0, :], bank(1)[:, 0:NQ], vec_sb[:, 0:1], vec_sb[:, 1:2], ALU.mult,
                            ALU.add).then_inc(affine0x, 1)
            dve.wait_ge(affine0, 1)
            dve.wait_ge(affine0x, 1)
            split(0)
            weight_lo(1)
            weight_lo(2)
            dve.wait_ge(in_more, 32)
            norm_stats(pro, [x_all[:, t, :] for t in range(QT, TT)], X_AT + QT).then_inc(var_done, 1)
            dve.wait_ge(in_rope, 32)
            dve.wait_ge(in_rest, REST * 16)
            v.tensor_copy(flat(sel_head[:]), head_raw).then_inc(sel_done, 1)
            dve.wait_ge(sel_done, 1)
            for n, (pair, q_bank, v_banks) in enumerate(AHEAD_B):
                rotate(n, pair)
                rotate_sum(n)
                if n == 0:
                    norm_stats(pro, [c_rows[:, t, :] for t in range(KT, 4 * KT)], KT).then_inc(var_done, 1)
                if n == 1:
                    dve.wait_ge(x1_done, 1)
                    norm_stats(pro, [x_rows[:, t, :] for t in range(QT, TT)], X2_AT + QT).then_inc(var_done, 1)
                keys_lo(n)
                queries_lo(n, n, q_bank)
            dve.wait_ge(w_lo_done, 3)

            batch(0, first=True)
            with dve.Fori(1, B - 1) as b:
                batch(b)
            batch(B - 1, last=True)
            reciprocals(B - 1)

            for c in range(CHUNKS):
                def weigh_mid(f):
                    n = c * FT + f
                    dve.wait_ge(gelu_done, n + 1)
                    dve.wait_ge(cb_filled, c * E + f // 2 + 1)
                    after(dve, mid_hi_done, n - BUF + 1)
                    after(dve, mid_lo_done, n - BUF + 1)
                    v.tensor_tensor(mid[:, f % BUF, :], act_out[:, f % BUF, :], bank(COMB_B[(f // 2) % 2]),
                                    ALU.mult).then_inc(mid_done, 1)

                def finish(c):
                    dve.wait_ge(yTT_done, c + 1)
                    after(dve, stored, 16 * c)
                    t0 = c * CH // P
                    v.tensor_tensor(y_out, x_all[:, t0:t0 + CH // P, :],
                                    bank(TURNED_B).rearrange("p (t d) -> p t d", d=D), ALU.add).then_inc(final_done, 1)

                for f in range(FT):
                    weigh_mid(f)
                    if c == 0 and f == 0:
                        for k in range(4):
                            scale(B - 1, k, SPREAD_LAST_B)
                    if c == 0 and f == 1:
                        residual(B - 1)
                    if c == 0 and f == 2:
                        route(1, 0)
                    if c == 0 and f == ROUTE_AT[0]:
                        route(1, 1)
                    if c == 0 and f == ROUTE_AT[1]:
                        route(1, 2)
                    if c == 1 and f == 1:
                        finish(0)
                if c == 1:
                    finish(1)

        @block.gpsimd
        def _(pool):
            own = Chain(pool, pool_pro, 0)
            nc.gpsimd.memset(minus_half[:], -0.5).then_inc(const_done, 1)
            nc.gpsimd.memset(euler[:], float(np.exp(1.0))).then_inc(const_done, 1)
            pool.wait_ge(const_done, 2)

            def power(count, at, n, sem_in=var_done, sem_out=rstd_done):
                pool.wait_ge(sem_in, count)
                nc.gpsimd.tensor_tensor(rstd[:, at:at + n], var_eps[:, at:at + n], minus_half[:, at:at + n],
                                        ALU.pow).then_inc(sem_out, 1)

            def normalise(dst, src, t):
                return nc.gpsimd.tensor_scalar(dst, src, mv[:, t, 0:1], rstd[:, t:t + 1], ALU.subtract, ALU.mult)

            def add_keys(b, h):
                pool.wait_ge(clip_done, b * HEADS + h + 1)
                after(pool, ksum_done, b * HEADS + h)
                after(pool, sums_done, b * G + h // GH - 1)
                n = 2 * NQ
                nc.gpsimd.tensor_tensor(half_sum[:], e_clip[:, h % 4, 0:n], e_clip[:, h % 4, n:2 * n],
                                        ALU.add).then_inc(half_done, 1)
                pool.wait_ge(half_done, b * HEADS + h + 1)
                nc.gpsimd.tensor_tensor(key_sum[:, h % 8, :], half_sum[:, 0:NQ], half_sum[:, NQ:n],
                                        ALU.add).then_inc(ksum_done, 1)

            def batch(b, last=False):
                for h in range(HEADS):
                    add_keys(b, h)
                    if last and h == 4:
                        power(1, 0, ROUTES[0][1], rvar_done, rrstd_done)
                    if last and h == 11:
                        gap(0)

            def gap(r):
                t0, t1 = ROUTES[r]
                pool.wait_ge(gap_done, r + 1)
                nc.gpsimd.tensor_tensor(top[:, 1, t0:t1], euler[:, t0:t1], top[:, 0, t0:t1], ALU.pow).then_inc(gap_exp, 1)

            power(1, X_AT, QT)
            power(2, 0, KT)
            power(3, X2_AT, QT)
            power(4, X_AT + QT, TT - QT)
            pool.wait_ge(rstd_done, 4)
            for t in range(QT, TT):
                ins = normalise(x_rows[:, t, :], x_all[:, t, :], X_AT + t)
                if t < TT - 1:
                    own.put(ins)
            ins.then_inc(x1_done, 1)
            power(5, KT, 3 * KT)
            pool.wait_ge(rstd_done, 5)
            for t in range(KT, 4 * KT):
                own.put(normalise(c_rows[:, t, :], c_rows[:, t, :], t))
            power(6, X2_AT + QT, TT - QT)
            pool.wait_ge(rstd_done, 6)
            for t in range(QT, TT):
                ins = normalise(x_rows[:, t, :], x_rows[:, t, :], X2_AT + t)
                if t < TT - 1:
                    own.put(ins)
            ins.then_inc(more_done, 1)

            batch(0)
            with pool.Fori(1, B - 1) as b:
                batch(b)
            batch(B - 1, last=True)
            for n in range(CHUNKS * FT):
                f = n % FT
                if n == 2:
                    power(2, ROUTES[1][0], QT, rvar_done, rrstd_done)
                if n == ROUTE_AT[1]:
                    gap(1)
                pool.wait_ge(mid_hi_done, n + 1)
                after(pool, down_done, n - BUF + 1)
                nc.gpsimd.tensor_tensor(mid_lo[:, f % BUF, :], mid[:, f % BUF, :], mid_hi[:, f % BUF, :].bitcast(F32),
                                        ALU.subtract).then_inc(mid_lo_done, 1)


ROUTE_AT = (7, 9, 12)


def kernel(x, ctx_1024, L0_xattn_cos, L0_xattn_sin, L0_xattn_ln_lat_g, L0_xattn_ln_lat_b, L0_xattn_ln_ctx_g,
           L0_xattn_ln_ctx_b, L0_xattn_Wq, L0_xattn_Wkv, L0_xattn_Wo, L0_xattn_bo, L0_ffn_router_w, L0_ffn_w1,
           L0_ffn_b1, L0_ffn_w2, L0_ffn_b2):
    import concourse.bacc as bacc
    from concourse.bass_utils import run_bass_kernel_spmd

    f = lambda a: np.ascontiguousarray(a)
    wkv = np.asarray(L0_xattn_Wkv)
    wk = wkv[:, :INNER].reshape(D, G, 2, 2, 2, DH // 2).transpose(0, 1, 4, 3, 2, 5).reshape(D, INNER)
    arrays = {
        "x": f(x),
        "ctx_in": f(ctx_1024),
        "cos_t": f(np.tile(np.asarray(L0_xattn_cos).T, (GH, 1))),
        "sin_t": f(np.tile(np.asarray(L0_xattn_sin).T, (GH, 1))),
        "vecs": f(np.stack([np.asarray(a) for a in (L0_xattn_ln_lat_g, L0_xattn_ln_lat_b, L0_xattn_ln_ctx_g,
                                                     L0_xattn_ln_ctx_b)], axis=1)),
        "wk": f(wk),
        "wq": f(np.asarray(L0_xattn_Wq).reshape(D, HEADS, 2, DH // 2).transpose(0, 1, 3, 2).reshape(D, INNER)),
        "wv": f(wkv[:, INNER:]),
        "wo": f(L0_xattn_Wo),
        "bo": f(L0_xattn_bo),
        "router_t": f(np.asarray(L0_ffn_router_w).T),
        "w1_t": f(np.asarray(L0_ffn_w1).transpose(2, 0, 1).reshape(D, E * FF)),
        "b1_t": f(np.asarray(L0_ffn_b1).reshape(FT, P).T),
        "w2_t": f(np.asarray(L0_ffn_w2).transpose(0, 2, 1).reshape(FT, P, D).transpose(1, 0, 2).reshape(P, FT * D)),
        "b2": f(L0_ffn_b2),
        "consts": constants(),
    }
    nc = bacc.Bacc("TRN2", target_bir_lowering=False, num_devices=1)
    args = {n: nc.dram_tensor(n, a.shape, mybir.dt.from_np(a.dtype), kind="ExternalInput").ap()
            for n, a in arrays.items()}
    args["out"] = nc.dram_tensor("out", (B, NQ, D), F32, kind="ExternalOutput").ap()
    build(nc, **args)
    r = run_bass_kernel_spmd(nc, [arrays], core_ids=[0])
    return r.results[0]["out"]
```

```python
from contextlib import ExitStack

import numpy as np

import concourse.bass as bass
from concourse import mybir

F32 = mybir.dt.float32
F32R = mybir.dt.float32r
U32 = mybir.dt.uint32
ALU = mybir.AluOpType
ACT = mybir.ActivationFunctionType

P = 128
B = 4
NQ = 256
NK = 512
D = 128
HEADS = 16
DH = 64
INNER = HEADS * DH
G = 4
GH = HEADS // G
PAIRS = HEADS // 2
KT = NK // P
QT = NQ // P
TOK = B * NQ
TT = TOK // P
E = 8
FF = 256
FT = E * FF // P
CH = 512
CHUNKS = TOK // CH
EPS = 1e-5
CLIP = 11.0
E_MIN = float(np.exp(np.float32(-CLIP)))
E_MAX = float(np.exp(np.float32(CLIP)))
SCALE = DH ** -0.5

WK_HI, WK_LO, WQ_HI, WQ_LO, WV_HI, WV_LO = (INNER * n for n in range(6))
W1_HI, W1_LO, W2_HI, W2_LO = (E * FF * n for n in range(4))

C_ID = 0
C_SEL = C_ID + P
C_MINUS = C_SEL + G * 32
C_HEAD = C_MINUS + 1
C_EXP = C_HEAD + PAIRS * P
C_IOTA = C_EXP + E * P
C_ALL = C_IOTA + TT * E


def constants():
    c = np.zeros((P, C_ALL), np.float32)
    c[:, C_ID:C_ID + P] = np.eye(P, dtype=np.float32)
    for g in range(G):
        c[:, C_SEL + 32 * g + g] = 1
        c[:, C_SEL + 32 * g + G + g] = 1
    c[:, C_SEL + 2 * G:C_SEL + 32] = 1
    for h in range(HEADS):
        row, at = 32 * (h % GH) + h // GH, C_HEAD + (h // 2) * P + (h % 2) * DH
        c[row, at:at + DH] = 1
        c[row + G, at:at + DH] = 1
        c[row + G, C_MINUS] = -1
    for e in range(E):
        c[e, C_EXP + e * P:C_EXP + (e + 1) * P] = 1
        c[E + e, C_EXP + e * P:C_EXP + (e + 1) * P] = 1
    c[:, C_IOTA:] = np.tile(np.arange(E, dtype=np.float32), TT)
    return c


class Chain:

    def __init__(self, eng, sem, per_round):
        self.eng, self.sem, self.per, self.n, self.base = eng, sem, per_round, 0, 0

    def start(self, round_):
        self.base, self.n = round_ * self.per, 0

    def put(self, ins):
        self.n += 1
        ins.then_inc(self.sem, 1)

    def wait(self):
        self.eng.wait_ge(self.sem, self.base + self.n)

    def link(self, ins):
        self.put(ins)
        self.wait()

    def end(self):
        assert self.n == self.per, (self.n, self.per)


def after(eng, sem, count):
    if not isinstance(count, int) or count > 0:
        eng.wait_ge(sem, count)


WARM = (24, 14, 36)
REST = 9
ATTN = 3
AHEAD = 3
SPREAD_AT = (4, 5)
PROJECT_AT = 6
ROUTE_AT = (10, 11, 16)
FINISH_AT = 22
POOL_LO = (0, 2)
LAG = 4
BUF = 4
X_AT, SLOTS = KT, B * KT + TT


def x_slot(t):
    return X_AT + t


def c_slot(t):
    return t if t < KT else TT + t


ROUTES = ((0, TT // 2), (TT // 2, TT))
PIECES = ((0, CH // P), (CH // P, CH // P + QT), (CH // P + QT, TT))
MORE = (("c", KT, 2 * KT), ("x", QT, 3 * QT), ("x", 3 * QT, TT), ("c", 2 * KT, 3 * KT), ("c", 3 * KT, B * KT))


def build(nc, x, ctx_in, cos_t, sin_t, vecs, wk, wq, wv, wo, bo, router_t, w1_t, b1_t, w2_t, b2, consts, out):
    stack = ExitStack()
    k_scratch = nc.dram_tensor("k_scratch", [G, GH, P, NK], F32, kind="Internal").ap()
    q_scratch = nc.dram_tensor("q_scratch", [G, GH, DH, NQ], F32, kind="Internal").ap()
    with stack:
        def sb(name, shape, dt=F32):
            return stack.enter_context(nc.sbuf_tensor(name, shape, dt))

        def sem(name):
            return stack.enter_context(nc.semaphore(name))

        def flat(ap):
            return ap.rearrange("p a b -> p (a b)")

        w_split = sb("w_split", [P, 3 * E * FF], F32R)
        wo_sb = sb("wo_sb", [P, PAIRS, D])
        k_stack = sb("k_stack", [P, HEADS, NK], F32R)
        q_dup = sb("q_dup", [P, HEADS, NQ], F32R)
        q_lo = sb("q_lo", [P, PAIRS, NQ], F32R)
        v_sb = sb("v_sb", [P, KT, INNER])
        e_raw = sb("e_raw", [P, 2, KT * NQ])
        e_clip = sb("e_clip", [P, 4, KT * NQ])
        o_scaled = sb("o_scaled", [P, PAIRS, NQ])
        half_sum = sb("half_sum", [P, 2 * NQ])
        key_sum = sb("key_sum", [P, 8, NQ])
        rope_c = sb("rope_c", [P, 2, NK])
        rope_s = sb("rope_s", [P, 2, NK])
        k_hi = sb("k_hi", [P, 2, NK], F32R)
        k_lo = sb("k_lo", [P, 2, NK], F32R)
        q_hi = sb("q_hi", [P, 2, NQ], F32R)
        cT_all = sb("cT_all", [P, B, NK])
        xT_all = sb("xT_all", [P, B, NQ])
        cT_hi = sb("cT_hi", [P, NK], F32R)
        cT_lo = sb("cT_lo", [P, NK], F32R)
        xT_hi = sb("xT_hi", [P, NQ], F32R)
        xT_lo = sb("xT_lo", [P, NQ], F32R)
        o_sb = sb("o_sb", [P, PAIRS, NQ])
        recip = sb("recip", [P, NQ])
        recip_hi = sb("recip_hi", [P, NQ], F32R)
        recip_parts = sb("recip_parts", [P, NQ], F32R)
        x_all = sb("x_all", [P, TT, D])
        cos_sb = sb("cos_sb", [P, NK])
        sin_sb = sb("sin_sb", [P, NK])
        bo_sb = sb("bo_sb", [P, D])
        vec_sb = sb("vec_sb", [P, 4])
        b1_sb = sb("b1_sb", [P, FT])
        router_sb = sb("router_sb", [P, E])
        b2_sb = sb("b2_sb", [2 * E, D])
        ident = sb("ident", [P, P])
        sel_sum_minus = sb("sel_sum_minus", [P, G * 32 + 1])
        sel_sum = sel_sum_minus[:, 0:G * 32].rearrange("p (g m) -> p g m", m=32)
        minus = sel_sum_minus[:, G * 32:]
        sel_head = sb("sel_head", [P, PAIRS, P], F32R)
        iota = sb("iota", [P, TT, E])
        stats = sb("stats", [P, SLOTS, 6])
        mv = sb("mv", [P, SLOTS, 2])
        var_eps = sb("var_eps", [P, SLOTS])
        rstd = sb("rstd", [P, SLOTS])
        minus_half = sb("minus_half", [P, SLOTS])
        euler = sb("euler", [P, TT])
        logits = sb("logits", [P, TT, E])
        max8 = sb("max8", [P, TT, E])
        idx8 = sb("idx8", [P, TT, E], U32)
        idx_f = sb("idx_f", [P, TT, 2])
        top = sb("top", [P, 5, TT])
        one1 = sb("one1", [P, TT, E])
        one2 = sb("one2", [P, TT, E])
        comb = sb("comb", [P, TT, 2 * E])
        o_scaled_last = flat(e_clip[:, 0:2, :]).rearrange("p (a q) -> p a q", q=NQ)
        w_raw = e_clip
        head_raw = flat(o_sb[:, 0:4, :])
        c_rows = cT_all[:].rearrange("p a (t d) -> p (a t) d", d=D)
        x_rows = xT_all[:].rearrange("p a (t d) -> p (a t) d", d=D)
        w1_raw = flat(cT_all[:])
        w2_raw = (flat(rope_c[:]), flat(rope_s[:]))
        exp_raw = flat(k_lo[:])[0:2 * E, :].bitcast(F32)
        h_norm = flat(k_hi[:]).bitcast(F32).rearrange("p (t d) -> p t d", d=D)
        hT = flat(xT_all[:])
        hT_hi = flat(q_dup[:, 0:4, :])
        hT_lo = flat(q_dup[:, 4:8, :])
        combT = flat(k_stack[0:2 * E, 0:2, :])
        sel_exp = flat(k_stack[0:2 * E, 2:4, :])
        b2_hi = q_dup[0:2 * E, 8, 0:D]
        b2_lo = q_dup[0:2 * E, 8, D:2 * D]
        mid_hi = k_stack[:, 4:4 + BUF, :]
        mid_lo = flat(q_lo[:]).rearrange("p (b n) -> p b n", n=CH)
        w2_lo = flat(k_stack[:, 8:12, :])
        act_out = cT_all
        mid = [rope[:, n, :] for rope in (rope_c, rope_s) for n in range(2)]
        yT = e_raw[:, 0, 0:CH]
        y_out = e_raw[:, 1, 0:CH].rearrange("p (t d) -> p t d", d=D)

        ps = [stack.enter_context(nc.psum_tensor(f"ps{n}", [P, 2, 512], F32)) for n in range(4)]

        def bank(n):
            return ps[n // 2][:, n % 2, :]

        KEY_B, QUERY_B, VALUE_B = 3, 6, (7, 6)
        AHEAD_B = ((3, 2, (3, 6)), (0, 7, (3, 6)), (2, 7, (3, 2)))
        SPREAD_B, SPREAD_LAST_B, OUT_B = (5, 5, 5, 5), (5, 2, 3, 5), 5
        TURN_B = (5, 5, 5, 7, 7)
        COMB_B, UP_B, RESULT_B, TURNED_B = (1, 4), (6, 7), (0, 5), (2, 2, 3)
        ROUTE_B = (6, 3)

        in_ctx0 = sem("in_ctx0")
        in_x0 = sem("in_x0")
        in_first = sem("in_first")
        in_qkv = [sem(f"in_qkv{n}") for n in range(3)]
        in_rope = sem("in_rope")
        in_more = sem("in_more")
        in_rest = sem("in_rest")
        in_up = sem("in_up")
        in_down = sem("in_down")
        in_exp = sem("in_exp")
        w_hi_done = sem("w_hi_done")
        w_lo_done = sem("w_lo_done")
        wv_lo_done = sem("wv_lo_done")
        sel_done = sem("sel_done")
        const_done = sem("const_done")
        zeros_done = sem("zeros_done")
        dve_pro = sem("dve_pro")
        dve_rope = sem("dve_rope")
        var_done = sem("var_done")
        rstd_done = sem("rstd_done")
        norm0_done = sem("norm0_done")
        pool_pro = sem("pool_pro")
        more_done = sem("more_done")
        more_ctx_done = sem("more_ctx_done")
        turned0 = sem("turned0")
        turned = sem("turned")
        affine0 = sem("affine0")
        affine0x = sem("affine0x")
        affine = sem("affine")
        x_hi_done = sem("x_hi_done")
        c_hi_done = sem("c_hi_done")
        split_done = sem("split_done")
        k_filled = sem("k_filled")
        k_taken = sem("k_taken")
        rope_done = sem("rope_done")
        k_hi_done = sem("k_hi_done")
        k_lo_done = sem("k_lo_done")
        k_hi_stored = sem("k_hi_stored")
        k_lo_stored = sem("k_lo_stored")
        k_first = sem("k_first")
        k_loaded = [sem(f"k_loaded{g}") for g in range(G)]
        q_filled = sem("q_filled")
        q_hi_done = sem("q_hi_done")
        q_lo_done = sem("q_lo_done")
        q_stored = sem("q_stored")
        q_loaded = [sem(f"q_loaded{g}") for g in range(G)]
        v_filled = sem("v_filled")
        v_done = sem("v_done")
        scores_done = sem("scores_done")
        exp_done = sem("exp_done")
        clip_done = sem("clip_done")
        half_done = sem("half_done")
        ksum_done = sem("ksum_done")
        pv_done = sem("pv_done")
        pv_taken = sem("pv_taken")
        sums_done = sem("sums_done")
        dve_attn = sem("dve_attn")
        recip_done = sem("recip_done")
        spread_done = sem("spread_done")
        scaled_done = sem("scaled_done")
        y_done = sem("y_done")
        resid_done = sem("resid_done")
        dve_route = sem("dve_route")
        rvar_done = sem("rvar_done")
        rrstd_done = sem("rrstd_done")
        hn_done = sem("hn_done")
        hT_filled = sem("hT_filled")
        hT_done = sem("hT_done")
        hT_hi_done = sem("hT_hi_done")
        hT_lo_done = sem("hT_lo_done")
        logits_done = sem("logits_done")
        gap_done = sem("gap_done")
        gap_exp = sem("gap_exp")
        comb_done = sem("comb_done")
        combT_filled = sem("combT_filled")
        combT_done = sem("combT_done")
        b2_done = sem("b2_done")
        w12_hi_done = sem("w12_hi_done")
        w12_lo_done = sem("w12_lo_done")
        cb_filled = sem("cb_filled")
        up_done = sem("up_done")
        gelu_done = sem("gelu_done")
        mid_done = sem("mid_done")
        mid_hi_done = sem("mid_hi_done")
        mid_lo_done = sem("mid_lo_done")
        last_lo_done = sem("last_lo_done")
        down_done = sem("down_done")
        yT_done = sem("yT_done")
        yTT_done = sem("yTT_done")
        final_done = sem("final_done")
        stored = sem("stored")

        block = stack.enter_context(nc.Block())


        @block.sync
        def _(sp):
            sp.dma_start(c_rows[:, 0:KT, :], ctx_in[0].rearrange("(t p) d -> p t d", p=P)).then_inc(in_ctx0, 16)
            sp.dma_start(x_all[:, 0:QT, :], x[0].rearrange("(t p) d -> p t d", p=P)).then_inc(in_x0, 16)
            sp.dma_start(ident[:], consts[:, C_ID:C_ID + P]).then_inc(in_first, 16)
            sp.dma_start(vec_sb[:], vecs).then_inc(in_first, 16)
            sp.dma_start(w_raw[:, 0, :], wk).then_inc(in_qkv[0], 16)
            sp.dma_start(w_raw[:, 1, :], wq).then_inc(in_qkv[1], 16)
            sp.dma_start(cos_sb[:], cos_t).then_inc(in_rope, 16)
            sp.dma_start(sin_sb[:], sin_t).then_inc(in_rope, 16)
            sp.dma_start(w_raw[:, 2, :], wv).then_inc(in_qkv[2], 16)
            sp.dma_start(c_rows[:, KT:, :], ctx_in[1:].rearrange("b (t p) d -> p (b t) d", p=P)).then_inc(in_more, 16)
            sp.dma_start(x_all[:, QT:, :], x[1:].rearrange("b (t p) d -> p (b t) d", p=P)).then_inc(in_more, 16)
            rest = [
                (head_raw, consts[:, C_HEAD:C_HEAD + PAIRS * P]),
                (sel_sum_minus[:], consts[:, C_SEL:C_HEAD]),
                (wo_sb[:], wo.rearrange("(c p) n -> p c n", p=P)),
                (bo_sb[:], bo.partition_broadcast(P)),
                (iota[:].rearrange("p t e -> p (t e)"), consts[:, C_IOTA:C_IOTA + TT * E]),
                (b1_sb[:], b1_t), (router_sb[:], router_t), (b2_sb[0:E, :], b2), (b2_sb[E:2 * E, :], b2),
            ]
            for dst, src in rest:
                sp.dma_start(dst, src).then_inc(in_rest, 16)
            assert len(rest) == REST

            def move_group(n, g, first=False):
                def store_queries():
                    sp.wait_ge(q_hi_done, n + 1)
                    sp.dma_start(q_scratch[g].rearrange("(a h) d q -> (h d) a q", a=2),
                                 q_hi[:].bitcast(F32)).then_inc(q_stored, 16)

                if not first:
                    store_queries()
                for part, hi, ready, stored_ in ((k_hi, True, k_hi_done, k_hi_stored),
                                                 (k_lo, False, k_lo_done, k_lo_stored)):
                    sp.wait_ge(ready, n + 1)
                    for odd in range(2):
                        at = 0 if hi != bool(odd) else DH
                        dst = k_scratch[g].rearrange("(jj jo) r s -> jo jj r s", jo=2)[odd, :, at:at + DH, :]
                        sp.dma_start(dst.rearrange("jj (r x) s -> jj r (x s)", x=2),
                                     flat(part[DH * odd:DH * odd + DH, :, :]).bitcast(F32)).then_inc(stored_, 16)
                    if hi and first:
                        store_queries()
                heads = slice(g * GH, (g + 1) * GH)
                sp.wait_ge(q_stored, (n + 1) * 16)
                for side in range(2):
                    sp.dma_start(q_dup[DH * side:DH * side + DH, heads, :].bitcast(F32),
                                 q_scratch[g].rearrange("h d q -> d h q")).then_inc(q_loaded[g], 16)
                sp.wait_ge(k_hi_stored, (n + 1) * 32)
                sp.wait_ge(k_lo_stored, (n + 1) * 32)
                halves = 2 if first else 1
                w = GH // halves
                for half in range(halves):
                    sp.dma_start(k_stack[:, g * GH + half * w:g * GH + (half + 1) * w, :].bitcast(F32),
                                 k_scratch[g, half * w:(half + 1) * w].rearrange("h r s -> r h s")
                                 ).then_inc(k_loaded[g] if half == halves - 1 else k_first, 16)

            for n in range(AHEAD):
                move_group(n, n, first=(n == 0))
            with sp.Fori(0, B - 1) as b:
                for s in range(G):
                    move_group(b * G + AHEAD + s, (AHEAD + s) % G)
            sp.wait_ge(split_done, B)
            sp.wait_ge(c_hi_done, B)
            sp.dma_start(w1_raw, w1_t).then_inc(in_up, 16)
            move_group(B * G - 1, G - 1)
            for n in range(2):
                sp.dma_start(w2_raw[n], w2_t[:, n * 2 * NK:(n + 1) * 2 * NK]).then_inc(in_down, 16)
            sp.dma_start(exp_raw, consts[0:2 * E, C_EXP:C_EXP + E * P]).then_inc(in_exp, 16)
            for i, (t0, t1) in enumerate(PIECES):
                sp.wait_ge(final_done, i + 1)
                at = t0 % (CH // P)
                sp.dma_start(out[t0 // QT:t1 // QT].rearrange("b (t p) d -> p (b t) d", p=P),
                             y_out[:, at:at + t1 - t0, :]).then_inc(stored, 16)
            sp.wait_ge(stored, 16 * len(PIECES))

        @block.tensor
        def _(pe):
            mm = nc.tensor.matmul

            def three(dst, w, w_lo, m, m_lo, start=True, stop=True):
                mm(dst, w, m, start=start, stop=False)
                mm(dst, w_lo, m, start=False, stop=False)
                return mm(dst, w, m_lo, start=False, stop=stop)

            def turn(dst, rows):
                for t, row in enumerate(rows):
                    ins = nc.tensor.transpose(dst[:, t * P:(t + 1) * P], row, ident[:])
                return ins

            def keys(n, g, pair=KEY_B):
                if g == 0:
                    pe.wait_ge(split_done, nb_of(n) + 1)
                after(pe, v_done, 2 * n if pair == KEY_B else 0)
                for half in range(2):
                    at = (2 * g + half) * P
                    ins = three(ps[pair][:, half, :], w_split[:, WK_HI + at:WK_HI + at + P],
                                w_split[:, WK_LO + at:WK_LO + at + P], cT_hi[:], cT_lo[:])
                ins.then_inc(k_filled, 1)

            def queries(n, g, to=QUERY_B):
                for pair in range(2):
                    at = (2 * g + pair) * P
                    ins = three(bank(to)[:, pair * NQ:(pair + 1) * NQ], w_split[:, WQ_HI + at:WQ_HI + at + P],
                                w_split[:, WQ_LO + at:WQ_LO + at + P], xT_hi[:], xT_lo[:])
                ins.then_inc(q_filled, 1)

            def values(n, g, half, to=None):
                to = VALUE_B[half] if to is None else to
                w = GH * DH
                for t in range(2):
                    kt = 2 * half + t
                    ins = three(bank(to)[:, t * w:(t + 1) * w], cT_hi[:, kt * P:(kt + 1) * P],
                                cT_lo[:, kt * P:(kt + 1) * P], w_split[:, WV_HI + g * w:WV_HI + (g + 1) * w],
                                w_split[:, WV_LO + g * w:WV_LO + (g + 1) * w])
                ins.then_inc(v_filled, 1)

            def nb_of(n):
                return n // G if isinstance(n, int) else open_batch[0]

            open_batch = [None]

            def scores(b, h, first=False):
                g, odd = h // GH, h % 2
                if first and h == 0:
                    pe.wait_ge(k_first, 16)
                if h % GH == (2 if first and h < GH else 0):
                    pe.wait_ge(k_loaded[g], b * 16 + 16)
                if h % GH == 0:
                    pe.wait_ge(q_loaded[g], b * 32 + 32)
                    pe.wait_ge(q_lo_done, b * G + g + 1)
                after(pe, exp_done, b * HEADS + h - 1)
                hi_rows = slice(DH * odd, DH * odd + DH)
                for kt in range(KT):
                    dst = ps[h % 2][:, kt // 2, (kt % 2) * NQ:(kt % 2) * NQ + NQ]
                    keys_ = slice(kt * P, (kt + 1) * P)
                    mm(dst, k_stack[:, h, keys_], q_dup[:, h, :], start=True, stop=False)
                    ins = mm(dst, k_stack[hi_rows, h, keys_], q_lo[hi_rows, h // 2, :], start=False, stop=True)
                ins.then_inc(scores_done, 1)

            def weigh(b, pair):
                if pair % 2 == 0:
                    pe.wait_ge(v_done, b * 2 * G + pair + 2)
                pe.wait_ge(clip_done, b * HEADS + 2 * pair + 2)
                after(pe, pv_taken, b * PAIRS + pair)
                for kt in range(KT):
                    for odd in range(2):
                        h = 2 * pair + odd
                        ins = mm(bank(4)[DH * odd:DH * odd + DH, 0:NQ], v_sb[:, kt, h * DH:(h + 1) * DH],
                                 e_clip[:, h % 4, kt * NQ:(kt + 1) * NQ], start=(kt == 0), stop=(kt == KT - 1))
                ins.then_inc(pv_done, 1)

            def sums(b, g):
                pe.wait_ge(in_rest, REST * 16)
                pe.wait_ge(ksum_done, b * HEADS + (g + 1) * GH)
                if g == 0:
                    after(pe, resid_done, b)
                for j in range(GH):
                    ins = mm(bank(5)[32 * j:32 * j + 32, 0:NQ], sel_sum[:, g, :], key_sum[:, (g * GH + j) % 8, :],
                             start=(g == 0), stop=(g == G - 1))
                ins.then_inc(sums_done, 1)

            def spread(b, k, banks):
                if k == 0:
                    pe.wait_ge(sel_done, 1)
                    pe.wait_ge(recip_done, b + 1)
                again = [j for j in range(k) if banks[j] == banks[k]]
                if again:
                    pe.wait_ge(scaled_done, b * 4 + again[-1] + 1)
                for pair in (2 * k, 2 * k + 1):
                    dst = bank(banks[k])[:, (pair % 2) * NQ:(pair % 2) * NQ + NQ]
                    ins = mm(dst, sel_head[:, pair, :], recip_parts[:], start=True, stop=True)
                ins.then_inc(spread_done, 1)

            def project(b, scaled=o_scaled):
                pe.wait_ge(scaled_done, b * 4 + 4)
                for t in range(QT):
                    for pair in range(PAIRS):
                        ins = mm(bank(OUT_B)[:, t * D:(t + 1) * D], scaled[:, pair, t * P:(t + 1) * P],
                                 wo_sb[:, pair, :], start=(pair == 0), stop=(pair == PAIRS - 1))
                ins.then_inc(y_done, 1)

            def turn_more(i):
                if i < 3:
                    pe.wait_ge(more_done, (1, 2, 2)[i])
                else:
                    pe.wait_ge(more_ctx_done, i - 2)
                    pe.wait_ge(v_done, 2 * (AHEAD + 2) + 1)
                if i == 0:
                    pe.wait_ge(k_taken, AHEAD)
                elif i < 3:
                    pe.wait_ge(affine, i)
                rows, t0, t1 = MORE[i]
                src = c_rows if rows == "c" else x_rows
                turn(bank(TURN_B[i]), [src[:, t, :] for t in range(t0, t1)]).then_inc(turned, 1)

            def route(r, part):
                t0, t1 = ROUTES[r]
                tiles = range(t0, t1)
                if part == 0:
                    pe.wait_ge(hn_done, r + 1)
                    for i, t in enumerate(tiles):
                        ins = turn(bank(ROUTE_B[r])[:, i * P:], [h_norm[:, t, :]])
                    ins.then_inc(hT_filled, 1)
                if part == 1:
                    pe.wait_ge(hT_done, r + 1)
                    for i, t in enumerate(tiles):
                        ins = mm(bank(ROUTE_B[r])[:, i * E:(i + 1) * E], hT[:, t * P:(t + 1) * P], router_sb[:],
                                 start=True, stop=True)
                    ins.then_inc(logits_done, 1)
                if part == 2:
                    pe.wait_ge(comb_done, r + 1)
                    for i, t in enumerate(tiles):
                        ins = turn(bank(ROUTE_B[r])[0:2 * E, i * P:], [comb[:, t, :]])
                    ins.then_inc(combT_filled, 1)

            def batch(b, first=False, last=False):
                for p in range(PAIRS):
                    s, even = p // 2, p % 2 == 0
                    fill = not last or s == 0
                    n, g = b * G + AHEAD + s, (AHEAD + s) % G
                    open_batch[0] = b + 1
                    late = p == 2
                    if first and p == 0:
                        pe.wait_ge(k_taken, 2)
                    if p != 3 and not (first and p in (1, 2)):
                        scores(b, 2 * p, first)
                    if first and p == 0:
                        pe.wait_ge(v_done, 2 * AHEAD)
                        scores(b, 1)
                        scores(b, 2, first)
                        pe.wait_ge(q_lo_done, 3)
                    if first and p == 6:
                        pe.wait_ge(affine, 4)
                    if fill and even and not late:
                        keys(n, g)
                    if p == 4 and not last:
                        sums(b, 0)
                    if p == 4 and last:
                        project(b - 1)
                    if first and p == 1:
                        turn_more(0)
                    if (p or not first) and not (first and p == 3):
                        scores(b, 2 * p + 1)
                    if p == 4 and last:
                        sums(b, 0)
                    if first and p == 2:
                        weigh(b, p - 1)
                    if fill and even and late:
                        keys(n, g)
                    if p == 0 and not first:
                        weigh(b - 1, PAIRS - 1)
                        sums(b - 1, G - 1)
                    if first and p == 1:
                        weigh(b, 0)
                        pe.wait_ge(k_taken, n + 1)
                        queries(n, g)
                    if fill and not even:
                        pe.wait_ge(k_taken, n + 1)
                        if first and p == 7:
                            pe.wait_ge(affine, 5)
                        values(n, g, 0)
                    if p in (2, 3) and not first:
                        spread(b - 1, (1, 3)[p - 2], SPREAD_B)
                    if p > 2 or p > 0 and not first:
                        weigh(b, p - 1)
                    if p == 1 and not first:
                        spread(b - 1, 0, SPREAD_B)
                    if first and p in (1, 2):
                        turn_more(p)
                    if first and p == 3:
                        pe.wait_ge(affine, 3)
                    if not even and p > 3:
                        sums(b, (p - 3) // 2)
                    if p == 2:
                        scores(b, 2 * p + 2)
                        if first:
                            scores(b, 2 * p + 3)
                        if not first:
                            spread(b - 1, 2, SPREAD_B)
                    if fill and even and (p or not first):
                        pe.wait_ge(k_taken, n + 1)
                        if first and p == 6:
                            turn_more(4)
                        queries(n, g)
                    if first and p == 1:
                        scores(b, 2 * p + 2)
                    if fill and not even:
                        pe.wait_ge(q_lo_done, n + 1)
                        values(n, g, 1)
                    if p == 3 and not first and not last:
                        project(b - 1)
                    if first and p == 5:
                        turn_more(3)
                    if last and p in (3, 5, 6):
                        route(0, (3, 5, 6).index(p))

            def keep_warm(n, to):
                for _ in range(n):
                    mm(bank(to)[:, 0:NQ], recip_hi[:, 0:P], recip_hi[:], start=True, stop=True)

            pe.wait_ge(zeros_done, 1)
            keep_warm(WARM[0], 7)
            pe.wait_ge(in_first, 32)
            pe.wait_ge(norm0_done, 1)
            turn(bank(0), [c_rows[:, t, :] for t in range(KT)]).then_inc(turned0, 1)
            pe.wait_ge(norm0_done, 2)
            turn(bank(1), [x_rows[:, t, :] for t in range(QT)]).then_inc(turned0, 1)
            keep_warm(WARM[1], 7)
            pe.wait_ge(w_lo_done, 1)
            for n, (pair, q_bank, v_banks) in enumerate(AHEAD_B):
                keys(n, n, pair)
            pe.wait_ge(w_lo_done, 2)
            queries(0, 0, AHEAD_B[0][1])
            pe.wait_ge(wv_lo_done, 1)
            pe.wait_ge(k_taken, 1)
            for n, (pair, q_bank, v_banks) in enumerate(AHEAD_B):
                after(pe, v_done, 2 * n - 1)
                values(n, n, 0, v_banks[0])
                if n == 0:
                    queries(1, 1, AHEAD_B[1][1])
                if n == 1:
                    pe.wait_ge(v_done, 2)
                if n == 2:
                    pe.wait_ge(q_lo_done, 1)
                values(n, n, 1, v_banks[1])
            pe.wait_ge(v_done, 2 * AHEAD - 1)
            keep_warm(WARM[2], 3)
            pe.wait_ge(q_lo_done, 2)
            queries(2, 2, AHEAD_B[2][1])

            batch(0, first=True)
            with pe.Fori(1, B - 1) as b:
                batch(b)
            batch(B - 1, last=True)

            def spread_weights(m):
                c, e = divmod(m, E)
                after(pe, mid_done, 2 * m - 2)
                if e == 0:
                    pe.wait_ge(combT_done, c + 1)
                if m == 1:
                    pe.wait_ge(pv_taken, B * PAIRS)
                mm(bank(COMB_B[m % 2]), sel_exp[:, e * P:(e + 1) * P], combT[:, c * CH:(c + 1) * CH],
                   start=True, stop=True).then_inc(cb_filled, 1)

            def up(n):
                c, f = divmod(n, FT)
                tok = slice(c * CH, (c + 1) * CH)
                if f == 0:
                    pe.wait_ge(hT_lo_done, c + 1)
                    pe.wait_ge(hT_hi_done, c + 1)
                if n == 0:
                    pe.wait_ge(combT_done, 1)
                after(pe, gelu_done, n - 1)
                three(bank(UP_B[n % 2]), w_split[:, W1_HI + f * P:W1_HI + (f + 1) * P],
                      w_split[:, W1_LO + f * P:W1_LO + (f + 1) * P],
                      hT_hi[:, tok], hT_lo[:, tok]).then_inc(up_done, 1)
                if n % 2 == 0 and f > 0:
                    spread_weights(n // 2)

            def down(n):
                c, f = divmod(n, FT)
                if f == 0:
                    if c:
                        pe.wait_ge(resid_done, B)
                    tok = slice(c * CH, (c + 1) * CH)
                    mm(bank(RESULT_B[c]), b2_hi, combT[:, tok], start=True, stop=False)
                    mm(bank(RESULT_B[c]), b2_lo, combT[:, tok], start=False, stop=False)
                hi = w_split[:, W2_HI + f * P:W2_HI + (f + 1) * P]
                pe.wait_ge(mid_hi_done, n + 1)
                mm(bank(RESULT_B[c]), hi, mid_hi[:, n % BUF, :], start=False, stop=False)
                mm(bank(RESULT_B[c]), w2_lo[:, f * P:(f + 1) * P], mid_hi[:, n % BUF, :], start=False, stop=False)
                if n < CHUNKS * FT - 1:
                    pe.wait_ge(mid_lo_done, n + 1)
                else:
                    pe.wait_ge(last_lo_done, 1)
                mm(bank(RESULT_B[c]), hi, mid_lo[:, n % BUF, :], start=False, stop=(f == FT - 1)).then_inc(down_done, 1)

            def turn_result(i):
                t0, t1 = PIECES[i]
                at = t0 % (CH // P)
                pe.wait_ge(yT_done, i + 1)
                if i == 1:
                    pe.wait_ge(final_done, 1)
                turn(bank(TURNED_B[i]), [yT[:, t * P:(t + 1) * P] for t in range(at, at + t1 - t0)]
                     ).then_inc(yTT_done, 1)

            pe.wait_ge(w12_hi_done, 2)
            pe.wait_ge(w12_lo_done, 2)
            up(0)
            up(1)
            weigh(B - 1, PAIRS - 1)
            pe.wait_ge(b2_done, 1)
            pe.wait_ge(exp_done, B * HEADS - 1)
            spread_weights(0)
            pe.wait_ge(w12_hi_done, 4)
            pe.wait_ge(w12_lo_done, 4)
            pe.wait_ge(exp_done, B * HEADS)
            for n in range(2, CHUNKS * FT + LAG):
                if n < CHUNKS * FT:
                    up(n)
                if n == PROJECT_AT + 1:
                    project(B - 1, o_scaled_last)
                if n == ROUTE_AT[2]:
                    route(1, 2)
                if n >= LAG:
                    down(n - LAG)
                if n == 2:
                    sums(B - 1, G - 1)
                if n == FT + 1:
                    spread_weights(E)
                if n in SPREAD_AT:
                    for k in (0, 1, 2) if n == SPREAD_AT[0] else (3,):
                        spread(B - 1, k, SPREAD_LAST_B)
                if n in ROUTE_AT[:2]:
                    route(1, ROUTE_AT.index(n))
                if n == FINISH_AT:
                    turn_result(0)
            for i in range(1, len(PIECES)):
                turn_result(i)

        @block.scalar
        def _(act):
            copy = nc.scalar.copy

            def affine_rows(dst, src, gain):
                return nc.scalar.activation(dst, src, ACT.Identity, bias=vec_sb[:, gain + 1:gain + 2],
                                            scale=vec_sb[:, gain:gain + 1])

            def latents_hi(nb):
                after(act, q_filled, nb * G)
                copy(xT_hi[:], xT_all[:, bass.ds(nb, 1), :].rearrange("p a k -> p (a k)")).then_inc(x_hi_done, 1)

            def context_hi(nb):
                after(act, v_filled, nb * 2 * G)
                copy(cT_hi[:], cT_all[:, bass.ds(nb, 1), :].rearrange("p a k -> p (a k)")).then_inc(c_hi_done, 1)

            def affine_more(i):
                rows, t0, t1 = MORE[i]
                act.wait_ge(turned, i + 1)
                dst = (cT_all if rows == "c" else xT_all)[:].rearrange("p b k -> p (b k)")
                affine_rows(dst[:, t0 * P:t1 * P], bank(TURN_B[i])[:, 0:(t1 - t0) * P],
                            2 if rows == "c" else 0).then_inc(affine, 1)

            def keys_hi(n):
                act.wait_ge(rope_done, n + 1)
                after(act, k_hi_stored, n * 32)
                copy(flat(k_hi[:]), flat(rope_c[:])).then_inc(k_hi_done, 1)

            def queries_hi(n, at=QUERY_B):
                act.wait_ge(q_filled, n + 1)
                after(act, q_stored, n * 16)
                copy(flat(q_hi[:]), bank(at)).then_inc(q_hi_done, 1)

            def values_out(n, g, half, at=None):
                at = VALUE_B[half] if at is None else at
                w = GH * DH
                act.wait_ge(v_filled, 2 * n + half + 1)
                copy(v_sb[:, 2 * half:2 * half + 2, g * w:(g + 1) * w],
                     bank(at).rearrange("p (t n) -> p t n", t=2)).then_inc(v_done, 1)

            def exps(b, h):
                act.wait_ge(scores_done, b * HEADS + h + 1)
                after(act, clip_done, b * HEADS + h - 1)
                nc.scalar.activation(e_raw[:, h % 2, :], flat(ps[h % 2][:, :, :]), ACT.Exp,
                                     scale=SCALE).then_inc(exp_done, 1)

            def take(b, pair):
                act.wait_ge(pv_done, b * PAIRS + pair + 1)
                after(act, scaled_done, (b - 1) * 4 + pair // 2 + 1)
                copy(o_sb[:, pair, :], bank(4)[:, 0:NQ]).then_inc(pv_taken, 1)

            def route(r, part):
                t0, t1 = ROUTES[r]
                cols = slice(t0 * P, t1 * P)
                if part == 1:
                    act.wait_ge(hT_done, r + 1)
                    copy(hT_hi[:, cols], hT[:, cols]).then_inc(hT_hi_done, 1)
                if part == 2:
                    act.wait_ge(combT_filled, r + 1)
                    w = (t1 - t0) * P
                    copy(combT[:, cols], bank(ROUTE_B[r])[0:2 * E, 0:w]).then_inc(combT_done, 1)

            def w12_hi(start, half, raw):
                at = start + half * 2 * NK
                copy(w_split[:, at:at + 2 * NK], raw).then_inc(w12_hi_done, 1)

            def batch(b, first=False, last=False):
                for p in range(PAIRS):
                    s, even = p // 2, p % 2 == 0
                    fill = not last or s == 0
                    n, g = b * G + AHEAD + s, (AHEAD + s) % G
                    if not (first and p == 3):
                        exps(b, 2 * p)
                    if first and p == 0:
                        queries_hi(2, AHEAD_B[2][1])
                    if p == 2 and not first:
                        take(b, 0)
                    exps(b, 2 * p + 1)
                    if first and p == 0:
                        keys_hi(2)
                    if p == 1 and not last and not first:
                        latents_hi(b + 1)
                        context_hi(b + 1)
                    if first and p == 1:
                        affine_more(0)
                        take(b, 0)
                        queries_hi(n)
                        affine_more(1)
                        act.wait_ge(affine, 2)
                        latents_hi(b + 1)
                        context_hi(b + 1)
                    if fill and not even:
                        values_out(n, g, 0)
                    if p == 0 and not first:
                        take(b - 1, PAIRS - 1)
                    if p > 1:
                        take(b, p - 1)
                    if first and p == 2:
                        affine_more(2)
                    if first and p == 2:
                        exps(b, 2 * p + 2)
                    if first and p == 6:
                        affine_more(4)
                    if fill and even and (p or not first):
                        queries_hi(n)
                        keys_hi(n)
                    if fill and not even:
                        values_out(n, g, 1)
                    if first and p == 1:
                        keys_hi(n)
                    if first and p == 5:
                        affine_more(3)
                    if last and p in (2, 3):
                        act.wait_ge(in_up, 16)
                        w12_hi(W1_HI, p - 2, w1_raw[:, (p - 2) * 2 * NK:(p - 1) * 2 * NK])
                    if last and p in (4, 5):
                        act.wait_ge(in_down, 32)
                        w12_hi(W2_HI, p - 4, w2_raw[p - 4])
                    if last and p == 4:
                        route(0, 1)
                    if last and p == 6:
                        route(0, 2)

            def weight_hi(i):
                act.wait_ge(in_qkv[i], 16)
                at = (WK_HI, WQ_HI, WV_HI)[i]
                copy(w_split[:, at:at + INNER], w_raw[:, i, :]).then_inc(w_hi_done, 1)

            weight_hi(0)
            act.wait_ge(in_first, 32)
            act.wait_ge(turned0, 1)
            affine_rows(cT_all[:, 0, :], bank(0), 2).then_inc(affine0, 1)
            act.wait_ge(affine0, 1)
            context_hi(0)
            act.wait_ge(affine0x, 1)
            latents_hi(0)
            weight_hi(1)
            weight_hi(2)
            keys_hi(0)
            queries_hi(0, AHEAD_B[0][1])
            for n, (pair, q_bank, v_banks) in enumerate(AHEAD_B):
                values_out(n, n, 0, v_banks[0])
                values_out(n, n, 1, v_banks[1])
            keys_hi(1)
            queries_hi(1, AHEAD_B[1][1])
            act.wait_ge(in_rest, REST * 16)
            copy(flat(sel_head[:]), head_raw).then_inc(sel_done, 1)

            batch(0, first=True)
            act.wait_ge(affine, 5)
            with act.Fori(1, B - 1) as b:
                batch(b)
            batch(B - 1, last=True)

            def gelu(n):
                f = n % FT
                act.wait_ge(up_done, n + 1)
                after(act, mid_done, n - BUF + 1)
                nc.scalar.activation(act_out[:, n % BUF, :], bank(UP_B[n % 2]), ACT.Gelu,
                                     bias=b1_sb[:, f:f + 1]).then_inc(gelu_done, 1)

            def part(n):
                act.wait_ge(mid_done, n + 1)
                after(act, down_done, n - BUF + 1)
                copy(mid_hi[:, n % BUF, :], mid[n % BUF]).then_inc(mid_hi_done, 1)

            def result(i):
                t0, t1 = PIECES[i]
                c = t0 * P // CH
                at, n = t0 * P % CH, (t1 - t0) * P
                act.wait_ge(down_done, (c + 1) * FT)
                if i == 1:
                    act.wait_ge(yTT_done, 1)
                copy(yT[:, at:at + n], bank(RESULT_B[c])[:, at:at + n]).then_inc(yT_done, 1)

            gelu(0)
            gelu(1)
            take(B - 1, PAIRS - 1)
            part(0)
            for n in range(2, CHUNKS * FT + 1):
                if n < CHUNKS * FT:
                    gelu(n)
                if n == ROUTE_AT[2]:
                    route(1, 2)
                part(n - 1)
                if n == ROUTE_AT[0]:
                    route(1, 1)
                if n == FINISH_AT - 1:
                    result(0)
            for i in range(1, len(PIECES)):
                result(i)

        @block.vector
        def _(dve):
            v = nc.vector
            pro = Chain(dve, dve_pro, 0)
            attn = Chain(dve, dve_attn, ATTN)
            rt = Chain(dve, dve_route, 0)

            def norm_stats(chain, rows, at, twice=False):
                n = len(rows)
                for t in range(n):
                    chain.put(v.bn_stats(stats[:, at + t, :], rows[t]))
                chain.wait()
                for t in range(n):
                    chain.put(v.bn_aggr(mv[:, at + t, :], stats[:, at + t, :]))
                chain.wait()
                if twice:
                    return v.tensor_scalar(var_eps[:, at:at + n], mv[:, at:at + n, 1], 1 + EPS, EPS * EPS,
                                           ALU.mult, ALU.add)
                return v.tensor_scalar(var_eps[:, at:at + n], mv[:, at:at + n, 1], EPS, None, ALU.add)

            def normalise(dst, src, t):
                return v.tensor_scalar(dst, src, mv[:, t, 0:1], rstd[:, t:t + 1], ALU.subtract, ALU.mult)

            def split(nb, context_first=False):
                after(dve, v_filled, nb * 2 * G)
                xs = xT_all[:, bass.ds(nb, 1), :].rearrange("p a k -> p (a k)")
                cs = cT_all[:, bass.ds(nb, 1), :].rearrange("p a k -> p (a k)")

                def latents():
                    dve.wait_ge(x_hi_done, nb + 1)
                    v.tensor_tensor(xT_lo[:], xs, xT_hi[:].bitcast(F32), ALU.subtract)

                def context():
                    dve.wait_ge(c_hi_done, nb + 1)
                    v.tensor_tensor(cT_lo[:], cs, cT_hi[:].bitcast(F32), ALU.subtract).then_inc(split_done, 1)

                if context_first:
                    context()
                    latents()
                else:
                    latents()
                    context()

            def rotate(n, pair=KEY_B):
                dve.wait_ge(k_filled, n + 1)
                after(dve, k_hi_done, n)
                after(dve, k_lo_done, n)
                both = ps[pair][:, :, :]
                v.tensor_tensor(rope_c[:], both, cos_sb[:].unsqueeze(1).to_broadcast([P, 2, NK]),
                                ALU.mult).then_inc(dve_rope, 1)
                v.tensor_tensor(rope_s[:], both, sin_sb[:].unsqueeze(1).to_broadcast([P, 2, NK]),
                                ALU.mult).then_inc(k_taken, 1)

            def rotate_sum(n):
                dve.wait_ge(dve_rope, 2 * n + 1)
                dve.wait_ge(k_taken, n + 1)
                v.tensor_tensor(rope_c[:, 0, :], rope_c[:, 0, :], rope_s[:, 1, :], ALU.subtract).then_inc(dve_rope, 1)
                v.tensor_tensor(rope_c[:, 1, :], rope_c[:, 1, :], rope_s[:, 0, :], ALU.add).then_inc(rope_done, 1)

            def keys_lo(n):
                dve.wait_ge(k_hi_done, n + 1)
                dve.wait_ge(rope_done, n + 1)
                after(dve, k_lo_stored, n * 32)
                v.tensor_tensor(flat(k_lo[:]), flat(rope_c[:]), flat(k_hi[:]).bitcast(F32),
                                ALU.subtract).then_inc(k_lo_done, 1)

            def queries_lo(n, g, at=QUERY_B):
                dve.wait_ge(q_hi_done, n + 1)
                v.tensor_tensor(flat(q_lo[:, 2 * g:2 * g + 2, :]), bank(at), flat(q_hi[:]).bitcast(F32),
                                ALU.subtract).then_inc(q_lo_done, 1)

            def clip(b, h):
                dve.wait_ge(exp_done, b * HEADS + h + 1)
                after(dve, pv_done, b * PAIRS + h // 2 - 1)
                after(dve, ksum_done, b * HEADS + h - 3)
                v.tensor_scalar(e_clip[:, h % 4, :], e_raw[:, h % 2, :], E_MIN, E_MAX, ALU.max,
                                ALU.min).then_inc(clip_done, 1)

            def reciprocals(b):
                attn.start(b)
                dve.wait_ge(sums_done, b * G + G)
                attn.link(v.reciprocal(recip[:], bank(5)[:, 0:NQ]))
                attn.link(v.tensor_copy(recip_hi[:], recip[:]))
                v.scalar_tensor_tensor(recip_parts[:], recip_hi[:].bitcast(F32), minus, recip[:], ALU.mult,
                                       ALU.add).then_inc(recip_done, 1)

            def scale(b, k, banks, scaled=o_scaled):
                dve.wait_ge(spread_done, b * 4 + k + 1)
                dve.wait_ge(pv_taken, b * PAIRS + PAIRS)
                if k == 0:
                    after(dve, y_done, b)
                    if scaled is o_scaled_last:
                        dve.wait_ge(pv_done, B * PAIRS)
                        dve.wait_ge(ksum_done, B * HEADS)
                v.tensor_tensor(flat(scaled[:, 2 * k:2 * k + 2, :]), bank(banks[k]),
                                flat(o_sb[:, 2 * k:2 * k + 2, :]), ALU.mult).then_inc(scaled_done, 1)

            def residual(b):
                dve.wait_ge(y_done, b + 1)
                rows = x_all[:, bass.ds(b * QT, QT), :]
                attn.link(v.tensor_tensor(rows, bank(OUT_B)[:, 0:QT * D].rearrange("p (t d) -> p t d", t=QT), rows,
                                          ALU.add))
                v.tensor_tensor(rows, rows, bo_sb[:].unsqueeze(1).to_broadcast([P, QT, D]), ALU.add).then_inc(resid_done, 1)
                attn.end()

            def route(r, part):
                t0, t1 = ROUTES[r]
                n = t1 - t0
                tiles, cols = slice(t0, t1), slice(t0 * P, t1 * P)
                if part == "stats":
                    dve.wait_ge(resid_done, (B // 2, B)[r])
                    norm_stats(rt, [x_all[:, t, :] for t in range(t0, t1)], t0).then_inc(rvar_done, 1)
                if part == "norm":
                    dve.wait_ge(k_hi_stored, B * G * 32)
                    dve.wait_ge(rrstd_done, r + 1)
                    for t in range(t0, t1):
                        ins = normalise(h_norm[:, t, :], x_all[:, t, :], t)
                        if t < t1 - 1:
                            rt.put(ins)
                    ins.then_inc(hn_done, 1)
                if part == "turned":
                    dve.wait_ge(hT_filled, r + 1)
                    v.tensor_copy(hT[:, cols], bank(ROUTE_B[r])[:, 0:n * P]).then_inc(hT_done, 1)
                if part == "split":
                    dve.wait_ge(hT_hi_done, r + 1)
                    dve.wait_ge(hT_done, r + 1)
                    v.tensor_tensor(hT_lo[:, cols], hT[:, cols], hT_hi[:, cols].bitcast(F32),
                                    ALU.subtract).then_inc(hT_lo_done, 1)
                if part == "choose":
                    dve.wait_ge(logits_done, r + 1)
                    rt.link(v.tensor_copy(logits[:, tiles, :].rearrange("p t e -> p (t e)"),
                                          bank(ROUTE_B[r])[:, 0:n * E]))
                    for t in range(t0, t1):
                        rt.put(v.max(max8[:, t, :], logits[:, t, :]))
                    rt.wait()
                    v.tensor_tensor(top[:, 0, tiles], max8[:, tiles, 1], max8[:, tiles, 0],
                                    ALU.subtract).then_inc(gap_done, 1)
                    for t in range(t0, t1):
                        rt.put(v.max_index(idx8[:, t, :], max8[:, t, :], logits[:, t, :]))
                    rt.wait()
                    rt.link(v.tensor_copy(idx_f[:, tiles, :], idx8[:, tiles, 0:2]))
                    for i, one in enumerate((one1, one2)):
                        rt.put(v.tensor_tensor(one[:, tiles, :], iota[:, tiles, :],
                                               idx_f[:, tiles, i:i + 1].to_broadcast([P, n, E]), ALU.is_equal))
                if part == "weigh":
                    dve.wait_ge(gap_exp, r + 1)
                    rt.link(v.tensor_scalar(top[:, 2, tiles], top[:, 1, tiles], 1.0, None, ALU.add))
                    rt.link(v.reciprocal(top[:, 3, tiles], top[:, 2, tiles]))
                    rt.link(v.tensor_tensor(top[:, 4, tiles], top[:, 1, tiles], top[:, 3, tiles], ALU.mult))
                    for i, one in enumerate((one1, one2)):
                        rt.put(v.tensor_tensor(one[:, tiles, :], one[:, tiles, :],
                                               top[:, 3 + i, tiles].unsqueeze(2).to_broadcast([P, n, E]), ALU.mult))
                    rt.wait()
                    rt.link(v.tensor_tensor(one1[:, tiles, :], one1[:, tiles, :], one2[:, tiles, :], ALU.add))
                    rt.link(v.tensor_copy(comb[:, tiles, 0:E].bitcast(F32R), one1[:, tiles, :]))
                    v.tensor_tensor(comb[:, tiles, E:2 * E], one1[:, tiles, :], comb[:, tiles, 0:E],
                                    ALU.subtract).then_inc(comb_done, 1)

            def normalise_context(b):
                dve.wait_ge(rstd_done, 5)
                for t in range(b * KT, (b + 1) * KT):
                    ins = normalise(c_rows[:, t, :], c_rows[:, t, :], c_slot(t))
                    if t < (b + 1) * KT - 1:
                        pro.put(ins)
                ins.then_inc(more_ctx_done, 1)

            def batch(b, first=False, last=False):
                for p in range(PAIRS):
                    s, even = p // 2, p % 2 == 0
                    fill = not last or s == 0
                    n, g = b * G + AHEAD + s, (AHEAD + s) % G
                    rotate_first = fill and p in (4, 6) or p == 0 and not first
                    if rotate_first:
                        rotate(n)
                    if p == 3 and not first:
                        scale(b - 1, 3, SPREAD_B)
                    if first and p == 1:
                        queries_lo(n, g)
                    clip(b, 2 * p)
                    if p == 2 and not first:
                        scale(b - 1, 1, SPREAD_B)
                    if first and p == 0:
                        clip(b, 1)
                        keys_lo(2)
                    if first and p == 3:
                        norm_stats(pro, [c_rows[:, t, :] for t in range(2 * KT, B * KT)],
                                   c_slot(2 * KT)).then_inc(var_done, 1)
                    if first and p == 5:
                        normalise_context(2)
                    if fill and even and not rotate_first:
                        rotate(n)
                    if p or not first:
                        clip(b, 2 * p + 1)
                    if first and p == 5:
                        normalise_context(3)
                    if fill and even:
                        rotate_sum(n)
                    if p == 2 and not first:
                        scale(b - 1, 2, SPREAD_B)
                    if p == 0 and not first:
                        reciprocals(b - 1)
                    if fill and even and (p or not first):
                        queries_lo(n, g)
                        if p not in POOL_LO:
                            keys_lo(n)
                    if p == 1 and not last:
                        if first:
                            dve.wait_ge(affine, 2)
                        split(b + 1)
                        if first:
                            keys_lo(n)
                    if p == 1 and not first:
                        scale(b - 1, 0, SPREAD_B)
                    if p == 3 and not first:
                        residual(b - 1)
                    if last and p == 1:
                        route(0, "stats")
                    if last and p == 2:
                        route(0, "norm")
                    if last and p == 3:
                        w12_lo(0, w_split[:, W1_LO:W1_LO + 2 * NK], w1_raw[:, 0:2 * NK], W1_HI)
                    if last and p == 4:
                        w12_lo(1, w_split[:, W1_LO + 2 * NK:W1_LO + 4 * NK], w1_raw[:, 2 * NK:], W1_HI + 2 * NK)
                        route(0, "turned")
                    if last and p == 5:
                        route(0, "split")
                        route(0, "choose")
                        route(0, "weigh")
                    if last and p in (6, 7):
                        half = p - 6
                        w12_lo(2 + half, w2_lo[:, half * 2 * NK:(half + 1) * 2 * NK], w2_raw[half],
                               W2_HI + half * 2 * NK)
                    if last and p == 6:
                        dve.wait_ge(in_exp, 16)
                        rt.put(v.tensor_copy(sel_exp, exp_raw))
                        rt.link(v.tensor_copy(b2_hi, b2_sb[:]))
                        v.tensor_tensor(b2_lo, b2_sb[:], b2_hi.bitcast(F32), ALU.subtract).then_inc(b2_done, 1)

            def w12_lo(i, dst, raw, hi):
                dve.wait_ge(w12_hi_done, i + 1)
                v.tensor_tensor(dst, raw, w_split[:, hi:hi + 2 * NK].bitcast(F32), ALU.subtract).then_inc(w12_lo_done, 1)

            def weight_lo(i):
                hi, lo = ((WK_HI, WK_LO), (WQ_HI, WQ_LO))[i]
                dve.wait_ge(w_hi_done, i + 1)
                v.tensor_tensor(w_split[:, lo:lo + INNER], w_raw[:, i, :], w_split[:, hi:hi + INNER].bitcast(F32),
                                ALU.subtract).then_inc(w_lo_done, 1)

            pro.link(v.memset(recip[:], 0.0))
            v.tensor_copy(recip_hi[:], recip[:]).then_inc(zeros_done, 1)
            dve.wait_ge(in_ctx0, 16)
            norm_stats(pro, [c_rows[:, t, :] for t in range(KT)], 0).then_inc(var_done, 1)
            dve.wait_ge(in_x0, 16)
            norm_stats(pro, [x_all[:, t, :] for t in range(QT)], X_AT, twice=True).then_inc(var_done, 1)
            dve.wait_ge(rstd_done, 1)
            for t in range(KT):
                ins = normalise(c_rows[:, t, :], c_rows[:, t, :], t)
                if t < KT - 1:
                    pro.put(ins)
            ins.then_inc(norm0_done, 1)
            dve.wait_ge(rstd_done, 2)
            for t in range(QT):
                ins = normalise(x_rows[:, t, :], x_all[:, t, :], x_slot(t))
                if t < QT - 1:
                    pro.put(ins)
            ins.then_inc(norm0_done, 1)
            weight_lo(0)
            dve.wait_ge(in_first, 32)
            dve.wait_ge(turned0, 2)
            v.tensor_scalar(xT_all[:, 0, :], bank(1)[:, 0:NQ], vec_sb[:, 0:1], vec_sb[:, 1:2], ALU.mult,
                            ALU.add).then_inc(affine0x, 1)
            dve.wait_ge(affine0, 1)
            dve.wait_ge(affine0x, 1)
            split(0, context_first=True)
            weight_lo(1)
            dve.wait_ge(in_rope, 32)
            rotate(0, AHEAD_B[0][0])
            rotate_sum(0)
            dve.wait_ge(in_more, 32)
            norm_stats(pro, [x_all[:, t, :] for t in range(QT, TT)], x_slot(QT), twice=True).then_inc(var_done, 1)
            keys_lo(0)
            queries_lo(0, 0, AHEAD_B[0][1])
            rotate(1, AHEAD_B[1][0])
            rotate_sum(1)
            norm_stats(pro, [c_rows[:, t, :] for t in range(KT, 2 * KT)], c_slot(KT)).then_inc(var_done, 1)
            keys_lo(1)
            queries_lo(1, 1, AHEAD_B[1][1])
            rotate(2, AHEAD_B[2][0])
            rotate_sum(2)
            queries_lo(2, 2, AHEAD_B[2][1])
            dve.wait_ge(w_lo_done, 2)
            dve.wait_ge(wv_lo_done, 1)

            batch(0, first=True)
            dve.wait_ge(affine, 5)
            with dve.Fori(1, B - 1) as b:
                batch(b)
            batch(B - 1, last=True)

            def weigh_mid(n):
                dve.wait_ge(gelu_done, n + 1)
                dve.wait_ge(cb_filled, n // 2 + 1)
                after(dve, mid_hi_done, n - BUF + 1)
                after(dve, mid_lo_done, n - BUF + 1)
                v.tensor_tensor(mid[n % BUF], act_out[:, n % BUF, :], bank(COMB_B[n // 2 % 2]),
                                ALU.mult).then_inc(mid_done, 1)

            def finish(i):
                t0, t1 = PIECES[i]
                at, n = t0 % (CH // P), t1 - t0
                dve.wait_ge(yTT_done, i + 1)
                if i == 1:
                    dve.wait_ge(stored, 16)
                v.tensor_tensor(y_out[:, at:at + n, :], x_all[:, t0:t1, :],
                                bank(TURNED_B[i])[:, 0:n * D].rearrange("p (t d) -> p t d", d=D),
                                ALU.add).then_inc(final_done, 1)

            for n in range(CHUNKS * FT):
                if n == SPREAD_AT[0]:
                    scale(B - 1, 0, SPREAD_LAST_B, o_scaled_last)
                if n == ROUTE_AT[0]:
                    route(1, "turned")
                weigh_mid(n)
                if n == 1:
                    reciprocals(B - 1)
                if n == SPREAD_AT[0]:
                    for k in (1, 2, 3):
                        scale(B - 1, k, SPREAD_LAST_B, o_scaled_last)
                if n == PROJECT_AT:
                    residual(B - 1)
                    route(1, "stats")
                if n == PROJECT_AT + 1:
                    route(1, "norm")
                if n == ROUTE_AT[1]:
                    route(1, "choose")
                if n == ROUTE_AT[1] + 1:
                    route(1, "split")
                    route(1, "weigh")
                if n == FINISH_AT:
                    finish(0)
            n = CHUNKS * FT - 1
            dve.wait_ge(mid_hi_done, n + 1)
            after(dve, down_done, n - BUF + 1)
            v.tensor_tensor(mid_lo[:, n % BUF, :], mid[n % BUF], mid_hi[:, n % BUF, :].bitcast(F32),
                            ALU.subtract).then_inc(last_lo_done, 1)
            for i in range(1, len(PIECES)):
                finish(i)

        @block.gpsimd
        def _(pool):
            own = Chain(pool, pool_pro, 0)
            nc.gpsimd.memset(minus_half[:], -0.5).then_inc(const_done, 1)
            nc.gpsimd.memset(euler[:], float(np.exp(1.0))).then_inc(const_done, 1)
            pool.wait_ge(const_done, 2)

            def power(count, at, n, sem_in=var_done, sem_out=rstd_done):
                pool.wait_ge(sem_in, count)
                nc.gpsimd.tensor_tensor(rstd[:, at:at + n], var_eps[:, at:at + n], minus_half[:, at:at + n],
                                        ALU.pow).then_inc(sem_out, 1)

            def normalise(dst, src, t):
                return nc.gpsimd.tensor_scalar(dst, src, mv[:, t, 0:1], rstd[:, t:t + 1], ALU.subtract, ALU.mult)

            def add_keys(b, h):
                pool.wait_ge(clip_done, b * HEADS + h + 1)
                after(pool, ksum_done, b * HEADS + h)
                after(pool, sums_done, b * G + h // GH - 1)
                n = 2 * NQ
                nc.gpsimd.tensor_tensor(half_sum[:], e_clip[:, h % 4, 0:n], e_clip[:, h % 4, n:2 * n],
                                        ALU.add).then_inc(half_done, 1)
                pool.wait_ge(half_done, b * HEADS + h + 1)
                nc.gpsimd.tensor_tensor(key_sum[:, h % 8, :], half_sum[:, 0:NQ], half_sum[:, NQ:n],
                                        ALU.add).then_inc(ksum_done, 1)

            def keys_lo(n):
                pool.wait_ge(k_hi_done, n + 1)
                pool.wait_ge(rope_done, n + 1)
                after(pool, k_lo_stored, n * 32)
                nc.gpsimd.tensor_tensor(flat(k_lo[:]), flat(rope_c[:]), flat(k_hi[:]).bitcast(F32),
                                        ALU.subtract).then_inc(k_lo_done, 1)

            def normalise_more(rows):
                for i, row in enumerate(rows):
                    ins = normalise(*row)
                    if i < len(rows) - 1:
                        own.put(ins)
                ins.then_inc(more_done, 1)

            def batch(b, first=False, last=False):
                for h in range(HEADS):
                    add_keys(b, h)
                    if h % 2 and h // 2 in POOL_LO and (h > 1 or not first) and (h == 1 or not last):
                        keys_lo(b * G + AHEAD + h // 4)
                    if first and h == 7:
                        power(5, c_slot(2 * KT), 2 * KT)
                    if last and h == 3:
                        power(1, 0, ROUTES[0][1], rvar_done, rrstd_done)
                    if last and h == 10:
                        gap(0)

            def gap(r):
                t0, t1 = ROUTES[r]
                pool.wait_ge(gap_done, r + 1)
                nc.gpsimd.tensor_tensor(top[:, 1, t0:t1], euler[:, t0:t1], top[:, 0, t0:t1], ALU.pow).then_inc(gap_exp, 1)

            power(1, 0, KT)
            power(2, X_AT, QT)
            pool.wait_ge(w_hi_done, 3)
            nc.gpsimd.tensor_tensor(w_split[:, WV_LO:WV_LO + INNER], w_raw[:, 2, :],
                                    w_split[:, WV_HI:WV_HI + INNER].bitcast(F32), ALU.subtract).then_inc(wv_lo_done, 1)
            power(3, x_slot(QT), TT - QT)
            power(4, c_slot(KT), KT)
            pool.wait_ge(rstd_done, 4)
            normalise_more([(c_rows[:, t, :], c_rows[:, t, :], c_slot(t)) for t in range(KT, 2 * KT)])
            normalise_more([(x_rows[:, t, :], x_all[:, t, :], x_slot(t)) for t in range(QT, TT)])

            batch(0, first=True)
            with pool.Fori(1, B - 1) as b:
                batch(b)
            batch(B - 1, last=True)
            for n in range(CHUNKS * FT):
                if n == PROJECT_AT + 1:
                    power(2, ROUTES[1][0], TT // 2, rvar_done, rrstd_done)
                if n == ROUTE_AT[1]:
                    gap(1)
                if n == CHUNKS * FT - 1:
                    break
                pool.wait_ge(mid_hi_done, n + 1)
                after(pool, down_done, n - BUF + 1)
                nc.gpsimd.tensor_tensor(mid_lo[:, n % BUF, :], mid[n % BUF], mid_hi[:, n % BUF, :].bitcast(F32),
                                        ALU.subtract).then_inc(mid_lo_done, 1)




def kernel(x, ctx_1024, L0_xattn_cos, L0_xattn_sin, L0_xattn_ln_lat_g, L0_xattn_ln_lat_b, L0_xattn_ln_ctx_g,
           L0_xattn_ln_ctx_b, L0_xattn_Wq, L0_xattn_Wkv, L0_xattn_Wo, L0_xattn_bo, L0_ffn_router_w, L0_ffn_w1,
           L0_ffn_b1, L0_ffn_w2, L0_ffn_b2):
    import concourse.bacc as bacc
    from concourse.bass_utils import run_bass_kernel_spmd

    f = lambda a: np.ascontiguousarray(a)
    wkv = np.asarray(L0_xattn_Wkv)
    wk = wkv[:, :INNER].reshape(D, G, 2, 2, 2, DH // 2).transpose(0, 1, 4, 3, 2, 5).reshape(D, INNER)
    arrays = {
        "x": f(x),
        "ctx_in": f(ctx_1024),
        "cos_t": f(np.tile(np.asarray(L0_xattn_cos).T, (GH, 1))),
        "sin_t": f(np.tile(np.asarray(L0_xattn_sin).T, (GH, 1))),
        "vecs": f(np.stack([np.asarray(a) for a in (L0_xattn_ln_lat_g, L0_xattn_ln_lat_b, L0_xattn_ln_ctx_g,
                                                     L0_xattn_ln_ctx_b)], axis=1)),
        "wk": f(wk),
        "wq": f(np.asarray(L0_xattn_Wq).reshape(D, HEADS, 2, DH // 2).transpose(0, 1, 3, 2).reshape(D, INNER)),
        "wv": f(wkv[:, INNER:]),
        "wo": f(L0_xattn_Wo),
        "bo": f(L0_xattn_bo),
        "router_t": f(np.asarray(L0_ffn_router_w).T),
        "w1_t": f(np.asarray(L0_ffn_w1).transpose(2, 0, 1).reshape(D, E * FF)),
        "b1_t": f(np.asarray(L0_ffn_b1).reshape(FT, P).T),
        "w2_t": f(np.asarray(L0_ffn_w2).transpose(0, 2, 1).reshape(FT, P, D).transpose(1, 0, 2).reshape(P, FT * D)),
        "b2": f(L0_ffn_b2),
        "consts": constants(),
    }
    nc = bacc.Bacc("TRN2", target_bir_lowering=False, num_devices=1)
    args = {n: nc.dram_tensor(n, a.shape, mybir.dt.from_np(a.dtype), kind="ExternalInput").ap()
            for n, a in arrays.items()}
    args["out"] = nc.dram_tensor("out", (B, NQ, D), F32, kind="ExternalOutput").ap()
    build(nc, **args)
    r = run_bass_kernel_spmd(nc, [arrays], core_ids=[0])
    return r.results[0]["out"]
```
